# Optimizing a Trainium2 kernel written in Bass

```python
import numpy as np
import jax
import jax.numpy as jnp

def _softmax(x, axis=-1):
    return jax.nn.softmax(x, axis=axis)

def _gelu(x):
    return jax.nn.gelu(x, approximate=True)

def _silu(x):
    return jax.nn.silu(x)

def _sigmoid(x):
    return jax.nn.sigmoid(x)

def _layernorm(x, axis=-1, eps=1e-05):
    m = jnp.mean(x, axis=axis, keepdims=True)
    v = jnp.var(x, axis=axis, keepdims=True)
    return (x - m) / jnp.sqrt(v + eps)

def _scatter_add(tgt, idx, src, axis=0):
    return tgt.at[idx].add(src)

def _segment_sum(src, seg, n):
    return jax.ops.segment_sum(src, seg, n)
kernel_name = 'mk_adaln_d1_jaxref_r8_a32c88'

def setup_inputs(seed: int=0):
    np.random.seed(seed)
    _w = jnp.asarray

    def _L0_attn_setup():
        import jax, jax.numpy as jnp
        import numpy as np
        HIDDEN = 512
        N_HEADS = 32
        KV_HEADS = 8
        HEAD_DIM = 128
        LOW_RANK = 64
        TOP_K_ROPE = 32
        ROPE_THETA = 10000.0
        B, S = (2, 256)
        GROUPS = N_HEADS // KV_HEADS
        _half = HEAD_DIM // 2
        _m = np.ones(_half, dtype=bool)
        _m[:TOP_K_ROPE] = False
        _m = np.concatenate([_m, _m])
        NOPE_MASK = np.tile(_m, KV_HEADS)
        ROPE_IDX = jnp.asarray(np.where(~NOPE_MASK)[0])
        NOPE_IDX = jnp.asarray(np.where(NOPE_MASK)[0])
        R_DIM = int((~NOPE_MASK).sum())
        C_DIM = LOW_RANK * KV_HEADS

        def _rope_tables(seq_len, dtype):
            inv_freq = 1.0 / ROPE_THETA ** (np.arange(0, HEAD_DIM, 2, dtype=np.float32) / HEAD_DIM)
            pos = np.arange(seq_len, dtype=np.float32)
            freqs = np.outer(pos, inv_freq)
            emb = np.concatenate([freqs, freqs], axis=-1)
            return (jnp.asarray(np.cos(emb), dtype), jnp.asarray(np.sin(emb), dtype))

        def _rotate_half(x):
            x1, x2 = (x[..., :HEAD_DIM // 2], x[..., HEAD_DIM // 2:])
            return jnp.concatenate([-x2, x1], axis=-1)
        key = jax.random.key(seed)
        ks = jax.random.split(key, 7)
        s = 0.02
        return {'hidden_states': jax.random.normal(ks[0], (B, S, HIDDEN), jnp.float32), 'Wq': jax.random.normal(ks[1], (N_HEADS * HEAD_DIM, HIDDEN), jnp.float32) * s, 'Wkr': jax.random.normal(ks[2], (R_DIM, HIDDEN), jnp.float32) * s, 'Wdk': jax.random.normal(ks[3], (C_DIM, HIDDEN), jnp.float32) * s, 'Wupk': jax.random.normal(ks[4], (KV_HEADS * HEAD_DIM - R_DIM, C_DIM), jnp.float32) * s, 'Wupv': jax.random.normal(ks[5], (KV_HEADS * HEAD_DIM, C_DIM), jnp.float32) * s, 'Wo': jax.random.normal(ks[6], (HIDDEN, N_HEADS * HEAD_DIM), jnp.float32) * s}
    _L0_attn_in = _L0_attn_setup()

    def _L0_ffn_setup():
        import jax, jax.numpy as jnp
        import numpy as np
        K_TOP = 8
        key = jax.random.key(seed)
        k1, k2, k3 = jax.random.split(key, 3)
        B, S, H, E = (4, 512, 512, 64)
        hidden_states = jax.random.normal(k1, (B, S, H), dtype=jnp.float32)
        router_weight = jax.random.normal(k2, (E, H), dtype=jnp.float32)
        router_bias = jnp.zeros((E,), dtype=jnp.float32)
        expert_bias = jax.random.normal(k3, (E, H), dtype=jnp.float32) * 0.1
        return {'hidden_states': hidden_states, 'router_weight': router_weight, 'router_bias': router_bias, 'expert_bias': expert_bias}
    _L0_ffn_in = _L0_ffn_setup()
    _L0_c = _w((lambda *s: np.random.randn(*s).astype(np.float32) * 0.05)(4, 512))
    _L0_wmod = _w((lambda *s: np.random.randn(*s).astype(np.float32) * 0.05)(512, 6 * 512) * 512 ** (-0.5))
    _d = {'L0_attn_hidden_states': _L0_attn_in['hidden_states'], 'L0_attn_Wq': _L0_attn_in['Wq'], 'L0_attn_Wkr': _L0_attn_in['Wkr'], 'L0_attn_Wdk': _L0_attn_in['Wdk'], 'L0_attn_Wupk': _L0_attn_in['Wupk'], 'L0_attn_Wupv': _L0_attn_in['Wupv'], 'L0_attn_Wo': _L0_attn_in['Wo'], 'L0_ffn_router_weight': _L0_ffn_in['router_weight'], 'L0_ffn_router_bias': _L0_ffn_in['router_bias'], 'L0_ffn_expert_bias': _L0_ffn_in['expert_bias'], 'L0_c': _L0_c, 'L0_wmod': _L0_wmod}
    _x0 = _d['L0_attn_hidden_states']
    _d['L0_attn_hidden_states'] = jax.random.normal(jax.random.fold_in(jax.random.key(seed), 1), (4, 512, 512), dtype=_x0.dtype)
    del _x0
    return _d

def reference(L0_attn_hidden_states, L0_attn_Wq, L0_attn_Wkr, L0_attn_Wdk, L0_attn_Wupk, L0_attn_Wupv, L0_attn_Wo, L0_ffn_router_weight, L0_ffn_router_bias, L0_ffn_expert_bias, L0_c, L0_wmod):

    def _L0_attn_ref(hidden_states, Wq, Wkr, Wdk, Wupk, Wupv, Wo):
        import jax, jax.numpy as jnp
        import numpy as np
        HIDDEN = 512
        N_HEADS = 32
        KV_HEADS = 8
        HEAD_DIM = 128
        LOW_RANK = 64
        TOP_K_ROPE = 32
        ROPE_THETA = 10000.0
        B, S = (2, 256)
        GROUPS = N_HEADS // KV_HEADS
        _half = HEAD_DIM // 2
        _m = np.ones(_half, dtype=bool)
        _m[:TOP_K_ROPE] = False
        _m = np.concatenate([_m, _m])
        NOPE_MASK = np.tile(_m, KV_HEADS)
        ROPE_IDX = jnp.asarray(np.where(~NOPE_MASK)[0])
        NOPE_IDX = jnp.asarray(np.where(NOPE_MASK)[0])
        R_DIM = int((~NOPE_MASK).sum())
        C_DIM = LOW_RANK * KV_HEADS

        def _rope_tables(seq_len, dtype):
            inv_freq = 1.0 / ROPE_THETA ** (np.arange(0, HEAD_DIM, 2, dtype=np.float32) / HEAD_DIM)
            pos = np.arange(seq_len, dtype=np.float32)
            freqs = np.outer(pos, inv_freq)
            emb = np.concatenate([freqs, freqs], axis=-1)
            return (jnp.asarray(np.cos(emb), dtype), jnp.asarray(np.sin(emb), dtype))

        def _rotate_half(x):
            x1, x2 = (x[..., :HEAD_DIM // 2], x[..., HEAD_DIM // 2:])
            return jnp.concatenate([-x2, x1], axis=-1)
        bsz, q_len, _ = hidden_states.shape
        dt = hidden_states.dtype
        q = (hidden_states @ Wq.T).reshape(bsz, q_len, N_HEADS, HEAD_DIM).transpose(0, 2, 1, 3)
        k_r0 = hidden_states @ Wkr.T
        key_flat = jnp.zeros((bsz, q_len, KV_HEADS * HEAD_DIM), dt).at[..., ROPE_IDX].set(k_r0)
        k = key_flat.reshape(bsz, q_len, KV_HEADS, HEAD_DIM).transpose(0, 2, 1, 3)
        cos, sin = _rope_tables(q_len, dt)
        cos, sin = (cos[None, None], sin[None, None])
        q = q * cos + _rotate_half(q) * sin
        k = k * cos + _rotate_half(k) * sin
        k_r = k.transpose(0, 2, 1, 3).reshape(bsz, q_len, KV_HEADS * HEAD_DIM)[..., ROPE_IDX]
        c_kv = hidden_states @ Wdk.T
        k_c = c_kv @ Wupk.T
        v = (c_kv @ Wupv.T).reshape(bsz, q_len, KV_HEADS, HEAD_DIM).transpose(0, 2, 1, 3)
        key_full = jnp.zeros((bsz, q_len, KV_HEADS * HEAD_DIM), dt).at[..., NOPE_IDX].set(k_c).at[..., ROPE_IDX].set(k_r)
        k = key_full.reshape(bsz, q_len, KV_HEADS, HEAD_DIM).transpose(0, 2, 1, 3)
        k = jnp.repeat(k, GROUPS, axis=1)
        v = jnp.repeat(v, GROUPS, axis=1)
        scale = 1.0 / jnp.sqrt(jnp.asarray(HEAD_DIM, dt))
        scores = jnp.einsum('bhqd,bhkd->bhqk', q, k) * scale
        causal = jnp.tril(jnp.ones((q_len, q_len), bool))
        scores = jnp.where(causal[None, None], scores, jnp.asarray(-1000000000.0, dt))
        attn = jax.nn.softmax(scores, axis=-1)
        out = jnp.einsum('bhqk,bhkd->bhqd', attn, v)
        out = out.transpose(0, 2, 1, 3).reshape(bsz, q_len, N_HEADS * HEAD_DIM)
        return out @ Wo.T

    def _L0_ffn_ref(hidden_states, router_weight, router_bias, expert_bias):
        import jax, jax.numpy as jnp
        import numpy as np
        K_TOP = 8
        B, S, H = hidden_states.shape
        E = router_weight.shape[0]
        T = B * S
        flat = hidden_states.reshape(T, H)
        logits = jnp.einsum('th,eh->te', flat, router_weight) + router_bias
        scores = jax.nn.softmax(logits, axis=-1)
        topk_w, topk_idx = jax.lax.top_k(scores, K_TOP)
        w_sum = topk_w.sum(axis=-1, keepdims=True)
        w_dense = jnp.zeros((T, E), dtype=scores.dtype).at[jnp.arange(T)[:, None], topk_idx].add(topk_w)
        bias_mix = jnp.einsum('te,eh->th', w_dense, expert_bias)
        out = flat * w_sum + bias_mix
        return out.reshape(B, S, H)
    x = L0_attn_hidden_states
    mod = (_silu(L0_c) @ L0_wmod).reshape(L0_c.shape[0], 6, 1, -1)
    sa, ca, ga, sb, cb, gb = (mod[:, 0], mod[:, 1], mod[:, 2], mod[:, 3], mod[:, 4], mod[:, 5])
    ga = (2 * (ga >= 0) - 1) * jnp.maximum(jnp.abs(ga), 0.25)
    gb = (2 * (gb >= 0) - 1) * jnp.maximum(jnp.abs(gb), 0.25)
    h = _layernorm(x, axis=-1) * (1 + ca) + sa
    x = x + ga * _L0_attn_ref(h, L0_attn_Wq, L0_attn_Wkr, L0_attn_Wdk, L0_attn_Wupk, L0_attn_Wupv, L0_attn_Wo)
    h = _layernorm(x, axis=-1) * (1 + cb) + sb
    x = x + gb * _L0_ffn_ref(h, L0_ffn_router_weight, L0_ffn_router_bias, L0_ffn_expert_bias)
    return x

_drawn_inputs = setup_inputs


def setup_inputs(seed=0):
    import zlib

    import numpy as np

    out = dict(_drawn_inputs(seed))
    spreads = {'L0_ffn_router_bias': (0.0, 2.0)}
    factors = {'L0_attn_Wq': 8.0,
     'L0_attn_Wkr': 8.0,
     'L0_attn_Wdk': 7.543,
     'L0_attn_Wupk': 8.0,
     'L0_attn_Wupv': 7.451,
     'L0_attn_Wo': 7.397,
     'L0_ffn_router_weight': 60.347,
     'L0_ffn_expert_bias': 59.908}
    for name, (base, spread) in spreads.items():
        noise = np.random.default_rng([zlib.crc32(name.encode()), seed]).standard_normal(out[name].shape)
        drawn = base * np.exp(spread * noise) if base else spread * noise
        out[name] = jnp.asarray(drawn.astype(out[name].dtype))
    for name, factor in factors.items():
        out[name] = (out[name] * factor).astype(out[name].dtype)
    return out
```

```python
from contextlib import ExitStack

import numpy as np

import concourse.bass as bass
from concourse import mybir

F32 = mybir.dt.float32
F32R = mybir.dt.float32r
ALU = mybir.AluOpType
ACT = mybir.ActivationFunctionType

P = 128
BATCH, SEQ, HID = 4, 512, 512
HEADS, KV, HD = 32, 8, 128
GROUP = HEADS // KV
LOW = 64
ROPE_HALF = 32
EXPERTS = 64
CH = HID // P
QT = SEQ // P
TILES = BATCH * QT
STEPS = BATCH * GROUP
NOPE = HD - 2 * ROPE_HALF
KVC = NOPE + HD
CAUSAL = P * QT * (QT + 1) // 2
SCALE = 1.0 / float(np.sqrt(np.float32(HD)))
EPS = 1e-5
MASKED = -1e30
LOWEST = -3e38

CHUNKS = ["wo0", "wo1", "wo2", "wo3", "wv", "wq0", "wk", "wq1", "wq2", "wq3"]
CHUNK_STEP = {1: [0, 1], 2: [2, 3], 10: [4, 5], 11: [6, 7], 12: [8], 13: [9]}
FIRST_CHUNKS = CHUNKS[4:]


def q_offset(qt):
    return P * qt * (qt + 1) // 2


KEY_ORDER = [0, 1, 3, 2]
KEY_OFFSET = {0: 0, 1: 512, 3: 896, 2: 1024}


class Mark:

    def __init__(self, ctx, nc, name, per=1, stride=STEPS, start=0):
        self.sem, self.per, self.stride, self.start = ctx.enter_context(nc.semaphore(name)), per, stride, start

    def up(self, instruction):
        instruction.then_inc(self.sem, 1)

    def wait(self, engine, t, n=None):
        g, k = t
        n = self.per if n is None else n
        constant = self.start + self.per * k + n
        if isinstance(g, int):
            value = self.per * self.stride * g + constant
            if value > 0:
                engine.wait_ge(self.sem, value)
        else:
            assert constant > 0
            engine.wait_ge(self.sem, g * (self.per * self.stride) + constant)


class Count:

    def __init__(self, ctx, nc, name):
        self.sem, self.value = ctx.enter_context(nc.semaphore(name)), 0

    def up(self, instruction, by=1):
        instruction.then_inc(self.sem, by)
        self.value += by
        return self.value

    def wait(self, engine, value=None):
        engine.wait_ge(self.sem, self.value if value is None else value)


def build(nc, A, out):
    pe, act, dve, pool, sp = nc.tensor, nc.scalar, nc.vector, nc.gpsimd, nc.sync
    ctx = ExitStack()
    with ctx:
        def mark(name, per=1, stride=STEPS, start=0):
            return Mark(ctx, nc, name, per, stride, start)

        def count(name):
            return Count(ctx, nc, name)

        base = (nc.sbuf_base + 63) // 64 * 64

        class Region:
            def __init__(self, start):
                self.at = start

            def take(self, name, shape, dt=F32):
                t = nc.alloc_sbuf_tensor_at(name, shape, dt, offset=self.at)
                self.at += (4 * int(np.prod(shape[1:])) + 31) // 32 * 32
                return t

        whole = Region(base)
        ident = whole.take("ident", [P, P])
        cos_t = whole.take("cos_t", [P, SEQ])
        sin_t = whole.take("sin_t", [P, SEQ])
        mask = whole.take("mask", [P, SEQ])
        y = whole.take("y", [P, TILES, HID])
        modT = whole.take("modT", [P, 2, CH, BATCH])
        stage = [whole.take(f"stage{i}", [P, HID]) for i in range(2)]
        attention_only = whole.at
        hT = [whole.take(f"hT_{p}", [P, BATCH * CH, SEQ], F32R) for p in ("hi", "lo")]
        wq = [whole.take(f"wq_{p}", [P, GROUP, CH, HD], F32R) for p in ("hi", "lo")]
        wk = [whole.take(f"wk_{p}", [P, CH, HD], F32R) for p in ("hi", "lo")]
        wv = [whole.take(f"wv_{p}", [P, CH, HD], F32R) for p in ("hi", "lo")]
        wo = [whole.take(f"wo_{p}", [P, GROUP, HID], F32R) for p in ("hi", "lo")]
        shared = whole.at
        OT = [whole.take(f"OT_{p}", [P, GROUP, SEQ], F32R) for p in ("hi", "lo")]
        PT = [whole.take(f"PT_{p}", [P, CAUSAL], F32R) for p in ("hi", "lo")]
        probs = [whole.take(f"probs{i}", [P, CAUSAL]) for i in range(2)]
        qT = [[whole.take(f"qT_{p}{i}", [P, SEQ], F32R) for p in ("hi", "lo")] for i in range(2)]
        kT = [whole.take(f"kT_{p}", [P, SEQ], F32R) for p in ("hi", "lo")]
        v = [whole.take(f"v_{p}", [P, QT, HD], F32R) for p in ("hi", "lo")]
        vT_raw = whole.take("vT_raw", [P, SEQ])
        wait_slot = whole.take("wait_slot", [P, QT])
        rot_c = whole.take("rot_c", [P, SEQ])
        rot_s = whole.take("rot_s", [P, SEQ])
        row_max, neg_max, row_sum, row_inv = (
            [whole.take(f"{n}{i}", [P, QT]) for i in range(2)] for n in ("row_max", "neg_max", "row_sum", "row_inv"))
        assert whole.at <= nc.sbuf_usable_end

        pro = Region(shared)
        c_in = pro.take("c_in", [P, CH, BATCH])
        c_exp = pro.take("c_exp", [P, CH, BATCH])
        c_silu = pro.take("c_silu", [P, CH, BATCH])
        wmod = [pro.take(f"wmod{i}", [P, CH, HID]) for i in range(2)]
        wdk = pro.take("wdk", [P, CH, HID])
        wup = [pro.take(f"wup{i}", [P, CH, 2 * KVC]) for i in range(2)]
        wc_out = [pro.take(f"wc_out{i}", [P, 2 * KVC]) for i in range(4)]
        h_raw = [pro.take(f"h_raw{i}", [P, SEQ]) for i in range(2)]
        stats = pro.take("stats", [P, QT, 6])
        mean_var = pro.take("mean_var", [P, TILES, 2])
        ve = pro.take("ve", [P, TILES])
        rstd = pro.take("rstd", [P, TILES])
        power = pro.take("power", [P, TILES])
        modrow = pro.take("modrow", [BATCH, 2, HID])
        gate_a = pro.take("gate_a", [BATCH, HID])
        gate_b = pro.take("gate_b", [BATCH, HID])
        modlate = pro.take("modlate", [BATCH, 2, HID])
        assert pro.at <= nc.sbuf_usable_end

        bank = {n: ctx.enter_context(nc.psum_tensor(f"bank_{n}", [P, 512], F32))
                for n in ("ta", "tb", "s3", "s2", "s1", "q", "pv", "x")}

        wc_d = nc.dram_tensor("wc_scratch", [KV, P, CH, KVC], F32).ap()
        mod_d = nc.dram_tensor("mod_scratch", [4, BATCH, HID], F32).ap()

        d_ident = count("d_ident")
        d_const, d_c, d_wdk = count("d_const"), count("d_c"), count("d_wdk")
        d_x = [count(f"d_x{b}") for b in range(BATCH)]
        d_wmod = [count(f"d_wmod{i}") for i in range(2)]
        d_wup = [count(f"d_wup{i}") for i in range(2)]
        d_wc = [count(f"d_wc{i}") for i in range(4)]
        d_mod = [count(f"d_mod{i}") for i in range(2)]
        pe_mod, pe_comb, pe_xt, pe_modT = count("pe_mod"), count("pe_comb"), count("pe_xt"), count("pe_modT")
        act_pro, act_comb, act_h = count("act_pro"), count("act_comb"), count("act_h")
        dve_pro, dve_mod, dve_ln, dve_xn, dve_h = (count("dve_pro"), count("dve_mod"), count("dve_ln"),
                                                   count("dve_xn"), count("dve_h"))
        pool_ln, pool_h = count("pool_ln"), count("pool_h")

        x_tiles = A["x"].rearrange("(b j p) n -> b p j n", p=P, j=QT)
        wmod_v = A["wmod"].rearrange("(c p) (j n) -> j p c n", p=P, n=HID)

        def load_wmod(j):
            if j >= 2:
                pe_mod.wait(sp, j - 1)
            d_wmod[j % 2].up(sp.dma_start(wmod[j % 2][:], wmod_v[j]), 16)

        def load_wup(n):
            if n >= 2:
                pe_comb.wait(act, CH * (n - 1))
            d_wup[n % 2].up(act.dma_start(wup[n % 2][:], A["wup"][n]), 16)

        d_c.up(sp.dma_start(c_in[:], A["c"]), 16)
        load_wmod(0)
        load_wmod(1)
        d_ident.up(sp.dma_start(ident[:], A["ident"]), 16)
        d_wdk.up(act.dma_start(wdk[:], A["wdk"].rearrange("(c p) n -> p c n", p=P)), 16)
        load_wup(0)
        for b in range(BATCH):
            d_x[b].up((sp if b < 2 else act).dma_start(y[:, QT * b:QT * b + QT, :], x_tiles[b]), 16)
        load_wup(1)

        d_c.wait(act)
        act_pro.up(act.activation(c_exp[:], c_in[:], ACT.Exp, scale=-1.0))
        act_pro.wait(dve)
        n = dve_pro.up(dve.tensor_scalar(c_exp[:], c_exp[:], 1.0, None, ALU.add))
        dve_pro.wait(dve, n)
        n = dve_pro.up(dve.reciprocal(c_exp[:], c_exp[:]))
        dve_pro.wait(dve, n)
        silu_ready = dve_pro.up(dve.tensor_tensor(c_silu[:], c_in[:], c_exp[:], ALU.mult))
        dve_pro.up(dve.memset(power[:], -0.5))
        power_ready = dve_pro.value

        def modulation(j):
            ps = bank["ta" if j % 2 == 0 else "tb"]
            dve_pro.wait(pe, silu_ready)
            pe.wait_ge(d_wmod[j % 2].sem, 16 * (j // 2 + 1))
            if j >= 2:
                dve_mod.wait(pe, mod_read[j - 2])
            for c in range(CH):
                mm = pe.matmul(ps[0:BATCH, :], c_silu[:, c, :], wmod[j % 2][:, c, :], start=(c == 0), stop=(c == CH - 1))
            pe_mod.up(mm)
            pe_mod.wait(dve, j + 1)
            where = modrow[:, j, :] if j < 2 else modlate[:, j % 2, :]
            if j >= 4:
                dve.wait_ge(d_mod[j % 2].sem, 16)
            if j in (0, 3):
                mod_read.append(dve_mod.up(dve.tensor_copy(where, ps[0:BATCH, :])))
            elif j in (1, 4):
                mod_read.append(dve_mod.up(dve.tensor_scalar(where, ps[0:BATCH, :], 1.0, None, ALU.add)))
            else:
                if j == 5:
                    dve_mod.wait(dve, gate_read[0])
                dve_mod.up(dve.tensor_scalar(gate_a[:], ps[0:BATCH, :], 0.0, 2.0, ALU.is_ge, ALU.mult))
                dve_mod.wait(dve)
                mod_read.append(dve_mod.up(dve.scalar_tensor_tensor(
                    out=gate_b[:], in0=gate_a[:], scalar=-1.0, in1=ps[0:BATCH, :], op0=ALU.add, op1=ALU.mult)))
                dve_mod.wait(dve)
                dve_mod.up(dve.tensor_scalar(gate_b[:], gate_b[:], 0.25, None, ALU.max))
                dve_mod.wait(dve)
                gate_read.append(dve_mod.up(dve.scalar_tensor_tensor(
                    out=where, in0=gate_a[:], scalar=-1.0, in1=gate_b[:], op0=ALU.add, op1=ALU.mult)))
            if j >= 2:
                dve_mod.wait(sp)
                d_mod[j % 2].up(sp.dma_start(mod_d[j - 2], where), 16)

        mod_read, gate_read = [], []
        modulation(0)
        modulation(1)
        dve_mod.wait(pe)
        d_ident.wait(pe)
        for j in range(2):
            for c in range(CH):
                o = (j * CH + c) * BATCH
                mm = pe.transpose(bank["q"][:, o:o + BATCH], modrow[:, j, c * P:(c + 1) * P], ident[0:BATCH, 0:BATCH])
        pe_modT.up(mm)
        pe_modT.wait(dve)
        modT_ready = dve_pro.up(dve.tensor_copy(modT[:].rearrange("p j c b -> p (j c b)"),
                                                bank["q"][:, 0:2 * CH * BATCH]))
        load_wmod(2)
        load_wmod(3)
        for dst, name in ((cos_t, "cos"), (sin_t, "sin"), (mask, "mask")):
            d_const.up(sp.dma_start(dst[:], A[name]), 16)

        def layer_norm(b):
            d_x[b].wait(dve)
            for j in range(QT):
                if b or j:
                    pass
                m = dve.bn_stats(stats[:, j, :], y[:, QT * b + j, :])
            dve_ln.up(m)
            dve_ln.wait(dve)
            for j in range(QT):
                m = dve.bn_aggr(mean_var[:, QT * b + j, :], stats[:, j, :])
            dve_ln.up(m)
            dve_ln.wait(pool)
            dve_pro.wait(pool, power_ready)
            s = slice(QT * b, QT * b + QT)
            n = pool_ln.up(pool.tensor_scalar(ve[:, s], mean_var[:, s, 1], EPS, None, ALU.add))
            pool_ln.wait(pool, n)
            n = pool_ln.up(pool.tensor_tensor(rstd[:, s], ve[:, s], power[:, s], ALU.pow))
            pool_ln.wait(dve, n)
            for j in range(QT):
                i = QT * b + j
                m = dve.tensor_scalar(y[:, i, :], y[:, i, :], mean_var[:, i, 0:1], rstd[:, i:i + 1],
                                      ALU.subtract, ALU.mult)
            return dve_xn.up(m)

        def transpose_h(b, ready):
            for c in range(CH):
                n = b * CH + c
                ps = bank["s1" if n % 2 == 0 else "pv"]
                dve_xn.wait(pe, ready)
                if n >= 2:
                    dve_h.wait(pe, n - 1)
                for j in range(QT):
                    mm = pe.transpose(ps[:, j * P:(j + 1) * P], y[:, QT * b + j, c * P:(c + 1) * P], ident[:])
                pe_xt.up(mm)
                pe_xt.wait(dve, n + 1)
                if n == 0:
                    dve_pro.wait(dve, modT_ready)
                if n >= 2:
                    pool_h.wait(dve, n - 1)
                dve_h.up(dve.tensor_scalar(h_raw[n % 2][:], ps[:], modT[:, 1, c, b:b + 1], modT[:, 0, c, b:b + 1],
                                           ALU.mult, ALU.add))
                dve_h.wait(act, n + 1)
                act_h.up(act.activation(hT[0][:, n, :], h_raw[n % 2][:], ACT.Copy))
                act_h.wait(pool, n + 1)
                pool_h.up(pool.tensor_tensor(hT[1][:, n, :], h_raw[n % 2][:], hT[0][:, n, :].bitcast(F32),
                                             ALU.subtract))

        def combine(n):
            d_wdk.wait(pe, 16)
            pe.wait_ge(d_wup[n % 2].sem, 16 * (n // 2 + 1))
            for c in range(CH):
                i = n * CH + c
                ps = bank["s3" if i % 2 == 0 else "s2"]
                if i >= 2:
                    act_comb.wait(pe, i - 1)
                for m in range(CH):
                    mm = pe.matmul(ps[:, 0:2 * KVC], wdk[:, m, c * P:(c + 1) * P], wup[n % 2][:, m, :],
                                   start=(m == 0), stop=(m == CH - 1))
                pe_comb.up(mm)
                pe_comb.wait(act, i + 1)
                if i >= 4:
                    act.wait_ge(d_wc[i % 4].sem, 16 * (i // 4))
                act_comb.up(act.activation(wc_out[i % 4][:], ps[:, 0:2 * KVC], ACT.Copy))
                act_comb.wait(sp, i + 1)
                d_wc[i % 4].up(sp.dma_start(wc_d[2 * n:2 * n + 2, :, c, :].rearrange("g p k -> p g k"),
                                            wc_out[i % 4][:].rearrange("p (g k) -> p g k", g=2)), 16)

        act_w = mark("act_w", 1, len(CHUNKS))
        pool_w = mark("pool_w", 1, len(CHUNKS))
        d_w = [ctx.enter_context(nc.semaphore(f"d_w{i}")) for i in range(2)]
        parts = [2 if c == "wk" else 1 for c in CHUNKS]
        FIRST = len(FIRST_CHUNKS)

        def chunk_event(i):
            return FIRST + i

        def dma_value(g, i):
            per = sum(parts[j] for j in range(i % 2, len(CHUNKS), 2))
            before = sum(parts[4 + j] for j in range(i % 2, FIRST, 2))
            local = sum(parts[j] for j in range(i % 2, i + 1, 2))
            return g * (16 * per) + 16 * (before + local)

        def first_dma_value(i):
            return 16 * sum(parts[4 + j] for j in range(i % 2, i + 1, 2))

        def chunk_load(g, name, slot, free):
            free()
            to = stage[slot]
            if name.startswith("wo"):
                src = A["wo"][bass.ts(g * GROUP + int(name[2]), P), :]
                sp.dma_start(to[:], src).then_inc(d_w[slot], 16)
            elif name.startswith("wq"):
                src = A["wq"][bass.ts(g * GROUP + int(name[2]), P), :]
                sp.dma_start(to[:], src).then_inc(d_w[slot], 16)
            elif name == "wv":
                src = wc_rows[bass.ts(g, P), :].rearrange("p (c k) -> p c k", c=CH)[:, :, NOPE:KVC]
                sp.dma_start(to[:].rearrange("p (c k) -> p c k", c=CH), src).then_inc(d_w[slot], 16)
            else:
                cols = to[:].rearrange("p (a k) -> p a k", k=2 * ROPE_HALF)
                rope = A["wkr"][bass.ts(g, P), :].rearrange("p (a k) -> p a k", k=ROPE_HALF)
                sp.dma_start(cols[:, :, 0:ROPE_HALF], rope).then_inc(d_w[slot], 16)
                nope = wc_rows[bass.ts(g, P), :].rearrange("p (c k) -> p c k", c=CH)[:, :, 0:NOPE]
                for_c = to[:].rearrange("p (c a k) -> p c a k", c=CH, a=2)[:, :, :, ROPE_HALF:2 * ROPE_HALF]
                sp.dma_start(for_c, nope.rearrange("p c (a k) -> p c a k", a=2)).then_inc(d_w[slot], 16)

        wc_rows = wc_d.rearrange("g p c k -> (g p) (c k)")

        def chunk_target(name):
            n = int(name[2]) if name[-1].isdigit() else 0
            flat = {"wo": lambda w: wo[w][:, n, :],
                    "wq": lambda w: wq[w][:, n].rearrange("p c d -> p (c d)"),
                    "wk": lambda w: wk[w][:].rearrange("p c d -> p (c d)"),
                    "wv": lambda w: wv[w][:].rearrange("p c d -> p (c d)")}[name[:2]]
            return flat(0), flat(1)

        def chunk_split(name, slot, landed, event, free):
            hi, lo = chunk_target(name)
            act.wait_ge(d_w[slot], landed)
            free()
            act_w.up(act.activation(hi, stage[slot][:], ACT.Copy))
            act_w.wait(pool, event)
            pool_w.up(pool.tensor_tensor(lo, stage[slot][:], hi.bitcast(F32), ALU.subtract))

        pe_t = mark("pe_t", 3)
        pe_s = mark("pe_s", 4)
        pe_qp = mark("pe_qp")
        pe_pv = mark("pe_pv")
        pe_v = mark("pe_v", 1, BATCH)
        pe_k = mark("pe_k", 1, BATCH)
        pe_vt = mark("pe_vt", 1, BATCH)
        pe_op = mark("pe_op", QT, BATCH)
        act_t = mark("act_t", 3)
        act_exp = mark("act_exp")
        act_norm = mark("act_norm")
        act_q = mark("act_q")
        act_o = mark("act_o")
        act_vraw = mark("act_vraw", 1, BATCH)
        act_v = mark("act_v", 1, BATCH)
        act_kn = mark("act_kn", 1, BATCH)
        act_k = mark("act_k", 1, BATCH)
        dve_t = mark("dve_t", 3)
        dve_s = mark("dve_s")
        dve_nm = mark("dve_nm")
        dve_ri = mark("dve_ri")
        dve_r = mark("dve_r")
        dve_o = mark("dve_o")
        dve_v = mark("dve_v", 1, BATCH)
        dve_kr = mark("dve_kr", 1, BATCH)
        dve_y = mark("dve_y", QT, BATCH, start=1)
        pool_a = mark("pool_a")
        pool_q = mark("pool_q")
        pool_ka = mark("pool_ka", 1, BATCH)
        pool_k = mark("pool_k", 1, BATCH)

        def passes(hi_lo_a, hi_lo_b):
            return [(hi_lo_a[0], hi_lo_b[1]), (hi_lo_a[1], hi_lo_b[0]), (hi_lo_a[0], hi_lo_b[0])]

        def unit_of(t):
            return t[0], t[1] // GROUP

        def before(t, n=1):
            return t[0], t[1] - n

        def q_proj(t):
            g, k = t
            b, h = (k // GROUP) % BATCH, k % GROUP
            dve_r.wait(pe, before(t))
            if b == 0:
                i = CHUNKS.index(f"wq{h}")
                shift = 0 if k < STEPS else 1
                pool_w.wait(pe, (g, len(CHUNKS) * (shift - 1) + chunk_event(i)), 1)
            for c in range(CH):
                for n, (w, x) in enumerate(passes(wq, hT)):
                    mm = pe.matmul(bank["q"][:], w[:, h, c, :], x[:, b * CH + c, :],
                                   start=(c == 0 and n == 0), stop=(c == CH - 1 and n == 2))
            pe_qp.up(mm)

        def q_rope(t, k_first=False):
            h = t[1] % GROUP
            pe_qp.wait(dve, t)
            pool_q.wait(dve, before(t))
            if h == 2 or k_first:
                pool_k.wait(dve, unit_of(t))
            dve.tensor_tensor(rot_c[:], bank["q"][:], cos_t[:], ALU.mult)
            dve.tensor_tensor(rot_s[0:64, :], bank["q"][64:128, :], sin_t[64:128, :], ALU.mult)
            dve_r.up(dve.tensor_tensor(rot_s[64:128, :], bank["q"][0:64, :], sin_t[0:64, :], ALU.mult))
            dve_r.wait(pool, t)
            pool_a.up(pool.tensor_tensor(rot_c[:], rot_c[:], rot_s[:], ALU.add))

        def q_split(t):
            hi, lo = qT[t[1] % 2]
            pool_a.wait(act, t)
            pe_s.wait(act, before(t, 2))
            act_q.up(act.activation(hi[:], rot_c[:], ACT.Copy))
            act_q.wait(pool, t)
            pool_q.up(pool.tensor_tensor(lo[:], rot_c[:], hi[:].bitcast(F32), ALU.subtract))

        def v_proj(u):
            g, b = u
            dve_y.wait(pe, before(u, 2))
            if b % BATCH == 0:
                shift = 0 if b < BATCH else 1
                pool_w.wait(pe, (g, len(CHUNKS) * (shift - 1) + chunk_event(CHUNKS.index("wv"))), 1)
            for c in range(CH):
                for n, (w, x) in enumerate(passes(wv, hT)):
                    mm = pe.matmul(bank["x"][:], w[:, c, :], x[:, (b % BATCH) * CH + c, :],
                                   start=(c == 0 and n == 0), stop=(c == CH - 1 and n == 2))
            pe_v.up(mm)
            pe_v.wait(act, u)
            act_vraw.up(act.activation(vT_raw[:], bank["x"][:], ACT.Copy))

        def k_proj(u):
            g, b = u
            act_vraw.wait(pe, u)
            if b % BATCH == 0:
                shift = 0 if b < BATCH else 1
                pool_w.wait(pe, (g, len(CHUNKS) * (shift - 1) + chunk_event(CHUNKS.index("wk"))), 1)
            for c in range(CH):
                for n, (w, x) in enumerate(passes(wk, hT)):
                    mm = pe.matmul(bank["x"][:], w[:, c, :], x[:, (b % BATCH) * CH + c, :],
                                   start=(c == 0 and n == 0), stop=(c == CH - 1 and n == 2))
            pe_k.up(mm)

        def k_rope(u, last_q):
            ps = bank["x"]
            pe_k.wait(dve, u)
            pool_q.wait(dve, last_q)
            dve.tensor_tensor(rot_c[:], ps[:], cos_t[:], ALU.mult)
            dve.tensor_tensor(rot_s[0:32, :], ps[64:96, :], sin_t[64:96, :], ALU.mult)
            dve_kr.up(dve.tensor_tensor(rot_s[64:96, :], ps[0:32, :], sin_t[0:32, :], ALU.mult))
            dve_kr.wait(pool, u)
            pool_ka.up(pool.tensor_tensor(rot_c[:], rot_c[:], rot_s[:], ALU.add))
            pool_ka.wait(act, u)
            act.activation(rot_c[32:64, :], ps[32:64, :], ACT.Copy)
            act_kn.up(act.activation(rot_c[96:128, :], ps[96:128, :], ACT.Copy))

        def k_split(u):
            act_kn.wait(act, u)
            pe_s.wait(act, (u[0], GROUP * u[1] - 1))
            act_k.up(act.activation(kT[0][:], rot_c[:], ACT.Copy))
            act_k.wait(pool, u)
            pool_k.up(pool.tensor_tensor(kT[1][:], rot_c[:], kT[0][:].bitcast(F32), ALU.subtract))

        def v_transpose(u):
            act_kn.wait(pe, u)
            act_vraw.wait(pe, u)
            for j in range(QT):
                mm = pe.transpose(bank["x"][:, j * P:(j + 1) * P], vT_raw[:, j * P:(j + 1) * P], ident[:])
            pe_vt.up(mm)

        def v_split(u):
            flat = [w[:].rearrange("p j d -> p (j d)") for w in v]
            pe_vt.wait(act, u)
            pe_pv.wait(act, (u[0], GROUP * u[1] - 1))
            act_v.up(act.activation(flat[0], bank["x"][:], ACT.Copy))
            act_v.wait(dve, u)
            dve_v.up(dve.tensor_tensor(flat[1], bank["x"][:], flat[0].bitcast(F32), ALU.subtract))

        score_bank = {3: bank["s3"][:, 0:512], 2: bank["s2"][:, 0:384], 1: bank["s1"][:, 0:256],
                      0: bank["s1"][:, 256:384]}
        QUERY_ORDER = [3, 2, 1, 0]

        def scores(t):
            pool_q.wait(pe, t)
            if t[1] % GROUP == 0:
                pool_k.wait(pe, unit_of(t))
            dve_s.wait(pe, before(t))
            for qt in QUERY_ORDER:
                for n, (q, k) in enumerate(passes(qT[t[1] % 2], kT)):
                    mm = pe.matmul(score_bank[qt], q[:, qt * P:(qt + 1) * P], k[:, 0:(qt + 1) * P],
                                   start=(n == 0), stop=(n == 2))
                pe_s.up(mm)

        def row(t, qt):
            return probs[t[1] % 2][:, q_offset(qt):q_offset(qt + 1)]

        def mask_and_max(t):
            m = t[1] % 2
            for n, qt in enumerate(QUERY_ORDER):
                if qt:
                    pe_s.wait(dve, t, 4 if qt == 1 else n + 1)
                    dve.memset(wait_slot[:, qt:qt + 1], 0.0)
                ins = dve.tensor_tensor_reduce(row(t, qt), score_bank[qt], mask[:, SEQ - (qt + 1) * P:], 1.0, LOWEST,
                                               ALU.add, ALU.max, row_max[m][:, qt:qt + 1])
            dve_s.up(ins)
            dve_s.wait(dve, t)
            dve_nm.up(dve.tensor_scalar(neg_max[m][:], row_max[m][:], -SCALE, None, ALU.mult))

        def exponentials(t):
            m = t[1] % 2
            dve_nm.wait(act, t)
            for qt in QUERY_ORDER:
                ins = act.activation(row(t, qt), row(t, qt), ACT.Exp, bias=neg_max[m][:, qt:qt + 1], scale=SCALE,
                                     accum_out=row_sum[m][:, qt:qt + 1])
            act_exp.up(ins)

        def invert_sums(t):
            m = t[1] % 2
            act_exp.wait(dve, t)
            dve_ri.up(dve.reciprocal(row_inv[m][:], row_sum[m][:]))

        def normalise(t):
            dve_ri.wait(act, t)
            for qt in QUERY_ORDER:
                ins = act.activation(row(t, qt), row(t, qt), ACT.Copy, scale=row_inv[t[1] % 2][:, qt:qt + 1])
            act_norm.up(ins)

        T_PARTS = [("ta", [0]), ("tb", [1, 3]), ("ta", [2])]

        def transpose_part(t, n):
            name, keys = T_PARTS[n]
            start = KEY_OFFSET[keys[0]]
            if n == 0:
                act_norm.wait(pe, t)
                dve_t.wait(pe, before(t))
            if n == 2:
                dve_t.wait(pe, t, 1)
            for kb in keys:
                for qt in range(kb, QT):
                    o = KEY_OFFSET[kb] - start + (qt - kb) * P
                    mm = pe.transpose(bank[name][:, o:o + P], row(t, qt)[:, kb * P:(kb + 1) * P], ident[:])
            pe_t.up(mm)

        def part_range(n):
            keys = T_PARTS[n][1]
            start = KEY_OFFSET[keys[0]]
            return start, sum((QT - kb) * P for kb in keys)

        def split_hi_part(t, n):
            at, size = part_range(n)
            pe_t.wait(act, t, n + 1)
            act_t.up(act.activation(PT[0][:, at:at + size], bank[T_PARTS[n][0]][:, 0:size], ACT.Copy))

        def split_lo_part(t, n):
            at, size = part_range(n)
            act_t.wait(dve, t, n + 1)
            dve_t.up(dve.tensor_tensor(PT[1][:, at:at + size], bank[T_PARTS[n][0]][:, 0:size],
                                       PT[0][:, at:at + size].bitcast(F32), ALU.subtract))

        def values(t, first_unit=False):
            h = t[1] % GROUP
            dve_t.wait(pe, t)
            if h == 0:
                dve_v.wait(pe, unit_of(t))
                dve_y.wait(pe, before(unit_of(t)), 3)
            else:
                dve_o.wait(pe, before(t))
            for kb in KEY_ORDER:
                for n, (a, p) in enumerate(passes(v, PT)):
                    mm = pe.matmul(bank["pv"][:, kb * P:SEQ], a[:, kb, :],
                                   p[:, KEY_OFFSET[kb]:KEY_OFFSET[kb] + (QT - kb) * P],
                                   start=(kb == 0 and n == 0), stop=(kb == KEY_ORDER[-1] and n == 2))
            pe_pv.up(mm)

        def o_split_hi(t):
            pe_pv.wait(act, t)
            act_o.up(act.activation(OT[0][:, t[1] % GROUP, :], bank["pv"][:], ACT.Copy))

        def o_split_lo(t):
            h = t[1] % GROUP
            act_o.wait(dve, t)
            dve_o.up(dve.tensor_tensor(OT[1][:, h, :], bank["pv"][:], OT[0][:, h, :].bitcast(F32), ALU.subtract))

        def out_proj(u, last=False):
            dve_o.wait(pe, (u[0], GROUP * u[1] + GROUP - 1))
            if u[1] == 0:
                pool_w.wait(pe, (u[0], chunk_event(3)), 1)
            for j in range(QT):
                ps = bank["pv" if j % 2 == 0 else "x"]
                if j == 1 and not last:
                    dve_v.wait(pe, (u[0], u[1] + 1))
                if j >= 2:
                    dve_y.wait(pe, u, j - 1)
                for h in range(GROUP):
                    for n, (o, w) in enumerate(passes(OT, wo)):
                        mm = pe.matmul(ps[:], o[:, h, j * P:(j + 1) * P], w[:, h, :],
                                       start=(h == 0 and n == 0), stop=(h == GROUP - 1 and n == 2))
                pe_op.up(mm)

        def add_out(u):
            for j in range(QT):
                ps = bank["pv" if j % 2 == 0 else "x"]
                i = (u[1] % BATCH) * QT + j
                pe_op.wait(dve, u, j + 1)
                dve_y.up(dve.tensor_tensor(y[:, i, :], ps[:], y[:, i, :], ALU.add))

        def step(g, k, last=False, first=False):
            t, u = (g, k), (g, k // GROUP)
            h = k % GROUP
            has1, has3 = not last or k + 1 < STEPS, not last or k + 3 < STEPS
            more = not last or u[1] + 1 < BATCH
            nxt1, nxt3, prev, un = (g, k + 1), (g, k + 3), (g, k - 1), (g, u[1] + 1)
            transpose_part(t, 0)
            transpose_part(t, 1)
            if not first:
                o_split_hi(prev)
                o_split_lo(prev)
            if h == 0:
                v_split(u)
            for n in (0, 1):
                split_hi_part(t, n)
                split_lo_part(t, n)
            if has1:
                scores(nxt1)
                mask_and_max(nxt1)
            transpose_part(t, 2)
            split_hi_part(t, 2)
            split_lo_part(t, 2)
            if has1:
                exponentials(nxt1)
                invert_sums(nxt1)
                normalise(nxt1)
            if has3:
                q_proj(nxt3)
                q_rope(nxt3)
                q_split(nxt3)
            if h == 0 and not first:
                out_proj(before(u))
                add_out(before(u))
            if more:
                if h == 1:
                    v_proj(un)
                elif h == 2:
                    k_proj(un)
                    k_rope(un, nxt3)
                    k_split(un)
                elif h == 3:
                    v_transpose(un)
            values(t)
            if k in CHUNK_STEP:
                for i in CHUNK_STEP[k]:
                    name = CHUNKS[i]
                    if last and i >= 4:
                        continue

                    def free(name=name):
                        if name[:2] == "wo":
                            pe_pv.wait(act, (g, 0))
                        elif name == "wv":
                            pe_v.wait(act, (g, BATCH - 1))
                        elif name == "wk":
                            pe_k.wait(act, (g, BATCH - 1))
                        else:
                            pe_qp.wait(act, (g, STEPS - GROUP + int(name[2])))
                    chunk_split(name, i % 2, dma_value(g, i), (g, chunk_event(i)), free)

        def group_loads(g, last=False):
            for i, name in enumerate(CHUNKS):
                if last and i >= 4:
                    break

                def stage_free(i=i):
                    pool_w.wait(sp, (g, chunk_event(i) - 2), 1)
                chunk_load(g if i < 4 else g + 1, name, i % 2, stage_free)

        ready = [layer_norm(0)]
        transpose_h(0, ready[0])
        combine(0)
        for b in range(1, BATCH):
            ready.append(layer_norm(b))
            transpose_h(b, ready[b])
            if b + 1 < BATCH:
                load_wup(b + 1)
            combine(b)
            modulation(b + 1)
            if b + 3 < 6:
                load_wmod(b + 3)
        modulation(5)
        pe_xt.wait(pool)
        dve_y.up(pool.memset(y[:], 0.0))

        for w in d_wc:
            w.wait(sp)
        for i, name in enumerate(FIRST_CHUNKS):
            def stage_free(i=i):
                if i >= 2:
                    pool_w.wait(sp, (0, i - 2), 1)
            chunk_load(0, name, i % 2, stage_free)
            chunk_split(name, i % 2, first_dma_value(i), (0, i), lambda: None)
        for e in (pe, act, dve, pool):
            pe_comb.wait(e)
            pe_mod.wait(e)
            pool_h.wait(e)
            act_comb.wait(e)
            for w in d_mod + d_wc:
                w.wait(e)
        rot_clear = dve_pro.up(dve.memset(rot_s[:], 0.0))
        dve_pro.wait(dve, rot_clear)
        d_const.wait(dve)
        dve_y.wait(dve, (0, -1))

        v_proj((0, 0))
        k_proj((0, 0))
        k_rope((0, 0), (0, -1))
        k_split((0, 0))
        v_transpose((0, 0))
        q_proj((0, 0))
        q_rope((0, 0), k_first=True)
        q_split((0, 0))
        scores((0, 0))
        mask_and_max((0, 0))
        exponentials((0, 0))
        invert_sums((0, 0))
        normalise((0, 0))
        for n in (1, 2):
            q_proj((0, n))
            q_rope((0, n))
            q_split((0, n))
        step(0, 0, first=True)

        with nc.Fori(0, KV - 1) as g:
            group_loads(g)
            for k in range(1, STEPS + 1):
                step(g, k)
        group_loads(KV - 1, last=True)
        for k in range(1, STEPS):
            step(KV - 1, k, last=True)
        final = (KV - 1, STEPS - 1)
        o_split_hi(final)
        o_split_lo(final)
        out_proj((KV - 1, BATCH - 1), last=True)
        add_out((KV - 1, BATCH - 1))

        ffn = Region(attention_only)
        gate1, shift2, scale2, gate2 = (
            [ffn.take(f"{n}{b}", [P, HID]) for b in range(BATCH)] for n in ("gate1_", "shift2_", "scale2_", "gate2_"))
        experts = ffn.take("experts", [EXPERTS, HID])
        router = ffn.take("router", [P, CH, EXPERTS])
        router_bias = ffn.take("router_bias", [P, EXPERTS])
        NB = 3
        x_in = [ffn.take(f"x_in{i}", [P, HID]) for i in range(NB)]
        h2 = [ffn.take(f"h2_{i}", [P, HID]) for i in range(NB)]
        h2T = [ffn.take(f"h2T_{i}", [P, CH, P]) for i in range(NB)]
        res = [ffn.take(f"res{i}", [P, HID]) for i in range(NB)]
        bn6 = [ffn.take(f"bn6_{i}", [P, 8]) for i in range(NB)]
        small = [ffn.take(f"small{i}", [P, 16]) for i in range(NB)]
        top8 = [ffn.take(f"top8_{i}", [P, 8]) for i in range(NB)]
        logit = [ffn.take(f"logit{i}", [P, EXPERTS]) for i in range(NB)]
        rest = [ffn.take(f"rest{i}", [P, EXPERTS]) for i in range(NB)]
        weight = [ffn.take(f"weight{i}", [P, EXPERTS]) for i in range(NB)]
        weightT = [ffn.take(f"weightT{i}", [EXPERTS, P]) for i in range(NB)]
        half = ffn.take("half", [P, 1])
        assert ffn.at <= nc.sbuf_usable_end

        d_ffn, d_xin, d_out = count("d_ffn"), [count(f"d_xin{i}") for i in range(NB)], [count(f"d_out{i}") for i in range(NB)]
        f = {n: count(f"f_{n}") for n in ("dve", "pool", "act", "pe")}
        dve_y.wait(sp, (KV - 1, BATCH - 1))
        pool_w.wait(sp, (KV - 1, chunk_event(3)), 1)
        for n, tiles in enumerate((gate1, shift2, scale2, gate2)):
            for b in range(BATCH):
                d_ffn.up(sp.dma_start(tiles[b][:], mod_d[n, b:b + 1, :].broadcast_to([P, HID])), 16)
        d_ffn.up(sp.dma_start(experts[:], A["eb"]), 16)
        d_ffn.up(sp.dma_start(router[:], A["rw"]), 16)
        d_ffn.up(sp.dma_start(router_bias[:], A["rb"].broadcast_to([P, EXPERTS])), 16)
        dve_y.wait(dve, (KV - 1, BATCH - 1))
        f["dve"].up(dve.memset(half[:], -0.5))
        for e in (dve, pool, pe, act):
            dve_y.wait(e, (KV - 1, BATCH - 1))
            d_ffn.wait(e)

        def self_wait(engine, name):
            f[name].wait(engine)

        x_rows = A["x"].rearrange("(i p) n -> i p n", p=P)
        out_rows = out.rearrange("(i p) n -> i p n", p=P)
        done = {}

        def load_x(i):
            if i >= NB:
                sp.wait_ge(f["dve"].sem, done[("x1", i - NB)])
            d_xin[i % NB].up(sp.dma_start(x_in[i % NB][:], x_rows[i]), 16)

        def ffn_norm(i):
            b, m = i // QT, i % NB
            load_x(i)
            yi, s = y[:, i, :], small[m]
            f["dve"].up(dve.tensor_tensor(yi, yi, gate1[b][:], ALU.mult))
            self_wait(dve, "dve")
            d_xin[m].wait(dve)
            done[("x1", i)] = f["dve"].up(dve.tensor_tensor(yi, yi, x_in[m][:], ALU.add))
            self_wait(dve, "dve")
            if i >= NB:
                dve.wait_ge(f["dve"].sem, done[("out", i - NB)])
            f["dve"].up(dve.bn_stats(bn6[m][:, 0:6], yi))
            self_wait(dve, "dve")
            f["dve"].up(dve.bn_aggr(s[:, 0:2], bn6[m][:, 0:6]))
            f["dve"].wait(pool)
            f["pool"].up(pool.tensor_scalar(s[:, 2:3], s[:, 1:2], EPS, None, ALU.add))
            self_wait(pool, "pool")
            f["pool"].up(pool.tensor_tensor(s[:, 3:4], s[:, 2:3], half[:], ALU.pow))
            f["pool"].wait(dve)
            if i >= NB:
                dve.wait_ge(f["pe"].sem, done[("h2T", i - NB)])
            f["dve"].up(dve.tensor_scalar(h2[m][:], yi, s[:, 0:1], s[:, 3:4], ALU.subtract, ALU.mult))
            f["dve"].wait(pool)
            f["pool"].up(pool.tensor_tensor(h2[m][:], h2[m][:], scale2[b][:], ALU.mult))
            self_wait(pool, "pool")
            done[("h2", i)] = f["pool"].up(pool.tensor_tensor(h2[m][:], h2[m][:], shift2[b][:], ALU.add))

        def ffn_router(i):
            m = i % NB
            ps, pl = bank["ta" if i % 2 == 0 else "tb"], bank["s3" if i % 2 == 0 else "s2"]
            pe.wait_ge(f["pool"].sem, done[("h2", i)])
            if i >= 2:
                pe.wait_ge(f["act"].sem, done[("h2T_copy", i - 2)])
                pe.wait_ge(f["dve"].sem, done[("logit", i - 2)])
            for c in range(CH):
                mm = pe.transpose(ps[:, c * P:(c + 1) * P], h2[m][:, c * P:(c + 1) * P], ident[:])
            done[("h2T", i)] = f["pe"].up(mm)
            f["pe"].wait(act)
            done[("h2T_copy", i)] = f["act"].up(act.activation(h2T[m][:].rearrange("p c t -> p (c t)"), ps[:], ACT.Copy))
            f["act"].wait(pe)
            for c in range(CH):
                mm = pe.matmul(pl[:, 0:EXPERTS], h2T[m][:, c, :], router[:, c, :], start=(c == 0), stop=(c == CH - 1))
            done[("logits_mm", i)] = f["pe"].up(mm)
            f["pe"].wait(dve)
            s = small[m]
            done[("logit", i)] = f["dve"].up(dve.tensor_tensor_reduce(
                logit[m][:], pl[:, 0:EXPERTS], router_bias[:], 1.0, LOWEST, ALU.add, ALU.max, s[:, 4:5]))
            self_wait(dve, "dve")
            f["dve"].up(dve.tensor_scalar(s[:, 5:6], s[:, 4:5], -1.0, None, ALU.mult))
            f["dve"].wait(act)
            f["act"].up(act.activation(logit[m][:], logit[m][:], ACT.Exp, bias=s[:, 5:6], accum_out=s[:, 6:7]))
            f["act"].wait(dve)
            f["dve"].up(dve.reciprocal(s[:, 7:8], s[:, 6:7]))
            f["dve"].up(dve.max(top8[m][:], logit[m][:]))
            self_wait(dve, "dve")
            f["dve"].up(dve.match_replace(rest[m][:], top8[m][:], logit[m][:], 0.0))
            self_wait(dve, "dve")
            f["dve"].up(dve.tensor_tensor(rest[m][:], logit[m][:], rest[m][:], ALU.subtract))
            self_wait(dve, "dve")
            if i >= NB:
                dve.wait_ge(f["pe"].sem, done[("mix", i - NB)])
            done[("weight", i)] = f["dve"].up(dve.tensor_scalar(
                weight[m][:], rest[m][:], s[:, 7:8], 0.0, ALU.mult, ALU.add, accum_out=s[:, 8:9]))

        def ffn_mix(i):
            b, m = i // QT, i % NB
            pw, px = bank["s1" if i % 2 == 0 else "q"], bank["pv" if i % 2 == 0 else "x"]
            pe.wait_ge(f["dve"].sem, done[("weight", i)])
            if i >= 2:
                pe.wait_ge(f["act"].sem, done[("wT", i - 2)])
                pe.wait_ge(f["dve"].sem, done[("mixed", i - 2)])
            f["pe"].up(pe.transpose(pw[0:EXPERTS, 0:P], weight[m][:], ident[:]))
            f["pe"].wait(act)
            done[("wT", i)] = f["act"].up(act.activation(weightT[m][:], pw[0:EXPERTS, 0:P], ACT.Copy))
            f["act"].wait(pe)
            done[("mix", i)] = f["pe"].up(pe.matmul(px[:], weightT[m][:], experts[:], start=True, stop=True))
            f["pe"].wait(dve)
            s = small[m]
            dve.wait_ge(f["pool"].sem, done[("h2", i)])
            if i >= NB:
                d_out[m].wait(dve)
            done[("mixed", i)] = f["dve"].up(dve.scalar_tensor_tensor(
                out=res[m][:], in0=h2[m][:], scalar=s[:, 8:9], in1=px[:], op0=ALU.mult, op1=ALU.add))
            f["dve"].wait(pool)
            f["pool"].up(pool.tensor_tensor(res[m][:], res[m][:], gate2[b][:], ALU.mult))
            f["pool"].wait(dve)
            done[("out", i)] = f["dve"].up(dve.tensor_tensor(res[m][:], res[m][:], y[:, i, :], ALU.add))
            f["dve"].wait(sp)
            d_out[m].up(sp.dma_start(out_rows[i], res[m][:]), 16)

        for i in range(TILES + 2):
            if i < TILES:
                ffn_norm(i)
            if 1 <= i <= TILES:
                ffn_router(i - 1)
            if i >= 2:
                ffn_mix(i - 2)
        for w in d_out:
            w.wait(sp)


def kernel(L0_attn_hidden_states, L0_attn_Wq, L0_attn_Wkr, L0_attn_Wdk, L0_attn_Wupk, L0_attn_Wupv, L0_attn_Wo,
           L0_ffn_router_weight, L0_ffn_router_bias, L0_ffn_expert_bias, L0_c, L0_wmod):
    import concourse.bacc as bacc
    from concourse.bass_utils import run_bass_kernel_spmd

    def lay(a, shape=None):
        a = np.ascontiguousarray(a)
        return a if shape is None else a.reshape(shape)

    upk = np.asarray(L0_attn_Wupk).reshape(KV, NOPE, HID)
    upv = np.asarray(L0_attn_Wupv).reshape(KV, HD, HID)
    up = np.concatenate([upk, upv], axis=1).reshape(KV // 2, 2 * KVC, CH, P).transpose(0, 3, 2, 1)
    inv_freq = 1.0 / 10000.0 ** (np.arange(0, HD, 2, dtype=np.float32) / HD)
    freqs = np.outer(np.arange(SEQ, dtype=np.float32), inv_freq)
    emb = np.concatenate([freqs, freqs], axis=-1)
    sign = np.concatenate([np.ones(HD // 2, np.float32), -np.ones(HD // 2, np.float32)])[:, None]
    causal = np.zeros((P, SEQ), np.float32)
    causal[:, SEQ - P:] = np.where(np.tril(np.ones((P, P), bool)), 0.0, MASKED)
    arrays = {
        "x": lay(L0_attn_hidden_states, (BATCH * SEQ, HID)),
        "c": lay(np.asarray(L0_c).T.reshape(CH, P, BATCH).transpose(1, 0, 2)),
        "wmod": lay(L0_wmod),
        "wq": lay(np.asarray(L0_attn_Wq).reshape(HEADS, HD, CH, P).transpose(0, 3, 2, 1), (HEADS * P, HID)),
        "wkr": lay(np.asarray(L0_attn_Wkr).reshape(KV, 2 * ROPE_HALF, CH, P).transpose(0, 3, 2, 1),
                   (KV * P, CH * 2 * ROPE_HALF)),
        "wdk": lay(L0_attn_Wdk),
        "wup": lay(up),
        "wo": lay(np.asarray(L0_attn_Wo).T),
        "rw": lay(np.asarray(L0_ffn_router_weight).T.reshape(CH, P, EXPERTS).transpose(1, 0, 2)),
        "rb": lay(L0_ffn_router_bias, (1, EXPERTS)),
        "eb": lay(L0_ffn_expert_bias),
        "cos": lay(np.cos(emb).astype(np.float32).T),
        "sin": lay(np.sin(emb).astype(np.float32).T * sign),
        "mask": causal,
        "ident": np.eye(P, dtype=np.float32),
    }
    nc = bacc.Bacc("TRN2", target_bir_lowering=False, num_devices=1)
    aps = {n: nc.dram_tensor(f"in_{n}", a.shape, F32, kind="ExternalInput").ap() for n, a in arrays.items()}
    out = nc.dram_tensor("out_y", (BATCH * SEQ, HID), F32, kind="ExternalOutput").ap()
    build(nc, aps, out)
    r = run_bass_kernel_spmd(nc, [{f"in_{n}": a for n, a in arrays.items()}], core_ids=[0])
    return r.results[0]["out_y"].reshape(BATCH, SEQ, HID)
```

```python
from contextlib import ExitStack

import numpy as np

import concourse.bass as bass
from concourse import mybir

F32 = mybir.dt.float32
F32R = mybir.dt.float32r
ALU = mybir.AluOpType
ACT = mybir.ActivationFunctionType

P = 128
BATCH, SEQ, HID = 4, 512, 512
HEADS, KV, HD = 32, 8, 128
GROUP = HEADS // KV
LOW = 64
ROPE_HALF = 32
EXPERTS = 64
CH = HID // P
QT = SEQ // P
TILES = BATCH * QT
STEPS = BATCH * GROUP
NOPE = HD - 2 * ROPE_HALF
KVC = NOPE + HD
CAUSAL = P * QT * (QT + 1) // 2
SCALE = 1.0 / float(np.sqrt(np.float32(HD)))
EPS = 1e-5
MASKED = -1e30
LOWEST = -3e38

CHUNKS = ["wo0", "wo1", "wo2", "wo3", "wk", "wq0", "wv", "wq1", "wq2", "wq3"]
CHUNK_STEP = {1: [0, 1], 2: [2], 3: [3], 10: [4, 5], 11: [6], 12: [7], 13: [8], 14: [9]}
HALVES = [(3, 2), (1, 0)]
FIRST_CHUNKS = CHUNKS[4:]


def q_offset(qt):
    return P * qt * (qt + 1) // 2


KEY_ORDER = [0, 1, 3, 2]
KEY_OFFSET = {0: 0, 1: 512, 3: 896, 2: 1024}


class Mark:

    def __init__(self, ctx, nc, name, per=1, stride=STEPS, start=0):
        self.sem, self.per, self.stride, self.start = ctx.enter_context(nc.semaphore(name)), per, stride, start

    def up(self, instruction):
        instruction.then_inc(self.sem, 1)

    def wait(self, engine, t, n=None):
        g, k = t
        n = self.per if n is None else n
        constant = self.start + self.per * k + n
        if isinstance(g, int):
            value = self.per * self.stride * g + constant
            if value > 0:
                engine.wait_ge(self.sem, value)
        else:
            assert constant > 0
            engine.wait_ge(self.sem, g * (self.per * self.stride) + constant)


class Count:

    def __init__(self, ctx, nc, name):
        self.sem, self.value = ctx.enter_context(nc.semaphore(name)), 0

    def up(self, instruction, by=1):
        instruction.then_inc(self.sem, by)
        self.value += by
        return self.value

    def wait(self, engine, value=None):
        engine.wait_ge(self.sem, self.value if value is None else value)


def build(nc, A, out):
    pe, act, dve, pool, sp = nc.tensor, nc.scalar, nc.vector, nc.gpsimd, nc.sync
    ctx = ExitStack()
    with ctx:
        def mark(name, per=1, stride=STEPS, start=0):
            return Mark(ctx, nc, name, per, stride, start)

        def count(name):
            return Count(ctx, nc, name)

        base = (nc.sbuf_base + 63) // 64 * 64

        class Region:
            def __init__(self, start):
                self.at = start

            def take(self, name, shape, dt=F32):
                t = nc.alloc_sbuf_tensor_at(name, shape, dt, offset=self.at)
                self.at += (4 * int(np.prod(shape[1:])) + 31) // 32 * 32
                return t

        whole = Region(base)
        ident = whole.take("ident", [P, P])
        cos_t = whole.take("cos_t", [P, SEQ])
        sin_t = whole.take("sin_t", [P, SEQ])
        mask = whole.take("mask", [P, SEQ])
        y = whole.take("y", [P, TILES, HID])
        modT = whole.take("modT", [P, 2, CH, BATCH])
        stage = [whole.take(f"stage{i}", [P, HID]) for i in range(2)]
        attention_only = whole.at
        hT = [whole.take(f"hT_{p}", [P, BATCH * CH, SEQ], F32R) for p in ("hi", "lo")]
        wq = [whole.take(f"wq_{p}", [P, GROUP, CH, HD], F32R) for p in ("hi", "lo")]
        wk = [whole.take(f"wk_{p}", [P, CH, HD], F32R) for p in ("hi", "lo")]
        wv = [whole.take(f"wv_{p}", [P, CH, HD], F32R) for p in ("hi", "lo")]
        wo = [whole.take(f"wo_{p}", [P, GROUP, HID], F32R) for p in ("hi", "lo")]
        shared = whole.at
        OT = [whole.take(f"OT_{p}", [P, GROUP, SEQ], F32R) for p in ("hi", "lo")]
        PT = [whole.take(f"PT_{p}", [P, CAUSAL], F32R) for p in ("hi", "lo")]
        probs = [whole.take(f"probs{i}", [P, CAUSAL]) for i in range(2)]
        qT = [[whole.take(f"qT_{p}{i}", [P, SEQ], F32R) for p in ("hi", "lo")] for i in range(2)]
        kT = [whole.take(f"kT_{p}", [P, SEQ], F32R) for p in ("hi", "lo")]
        v = [whole.take(f"v_{p}", [P, QT, HD], F32R) for p in ("hi", "lo")]
        kv_raw = whole.take("kv_raw", [P, SEQ])
        wait_slot = whole.take("wait_slot", [P, QT])
        rot_c = whole.take("rot_c", [P, SEQ])
        rot_s = whole.take("rot_s", [P, SEQ])
        row_max, neg_max, row_sum, row_inv = (
            [whole.take(f"{n}{i}", [P, QT]) for i in range(2)] for n in ("row_max", "neg_max", "row_sum", "row_inv"))
        assert whole.at <= nc.sbuf_usable_end

        pro = Region(shared)
        c_in = pro.take("c_in", [P, CH, BATCH])
        c_exp = pro.take("c_exp", [P, CH, BATCH])
        c_silu = pro.take("c_silu", [P, CH, BATCH])
        wmod = [pro.take(f"wmod{i}", [P, CH, HID]) for i in range(2)]
        wdk = pro.take("wdk", [P, CH, HID])
        wup = [pro.take(f"wup{i}", [P, CH, 2 * KVC]) for i in range(2)]
        wc_out = [pro.take(f"wc_out{i}", [P, 2 * KVC]) for i in range(4)]
        h_raw = [pro.take(f"h_raw{i}", [P, SEQ]) for i in range(2)]
        stats = pro.take("stats", [P, QT, 6])
        mean_var = pro.take("mean_var", [P, TILES, 2])
        ve = pro.take("ve", [P, TILES])
        rstd = pro.take("rstd", [P, TILES])
        power = pro.take("power", [P, TILES])
        modrow = pro.take("modrow", [BATCH, 2, HID])
        gate_a = pro.take("gate_a", [BATCH, HID])
        gate_b = pro.take("gate_b", [BATCH, HID])
        modlate = pro.take("modlate", [BATCH, 2, HID])
        assert pro.at <= nc.sbuf_usable_end

        bank = {n: ctx.enter_context(nc.psum_tensor(f"bank_{n}", [P, 512], F32))
                for n in ("ta", "tb", "s3", "s2", "s1", "q", "pv", "x")}

        wc_d = nc.dram_tensor("wc_scratch", [KV, P, CH, KVC], F32).ap()
        mod_d = nc.dram_tensor("mod_scratch", [4, BATCH, HID], F32).ap()

        d_ident = count("d_ident")
        d_const, d_c, d_wdk = count("d_const"), count("d_c"), count("d_wdk")
        d_x = [count(f"d_x{b}") for b in range(BATCH)]
        d_wmod = [count(f"d_wmod{i}") for i in range(2)]
        d_wup = [count(f"d_wup{i}") for i in range(2)]
        d_wc = [count(f"d_wc{i}") for i in range(4)]
        d_mod = [count(f"d_mod{i}") for i in range(2)]
        pe_mod, pe_comb, pe_xt, pe_modT = count("pe_mod"), count("pe_comb"), count("pe_xt"), count("pe_modT")
        act_pro, act_comb, act_h = count("act_pro"), count("act_comb"), count("act_h")
        dve_pro, dve_mod, dve_ln, dve_xn, dve_h = (count("dve_pro"), count("dve_mod"), count("dve_ln"),
                                                   count("dve_xn"), count("dve_h"))
        pool_ln, pool_h = count("pool_ln"), count("pool_h")

        x_tiles = A["x"].rearrange("(b j p) n -> b p j n", p=P, j=QT)
        wmod_v = A["wmod"].rearrange("(c p) (j n) -> j p c n", p=P, n=HID)

        def load_wmod(j):
            if j >= 2:
                pe_mod.wait(sp, j - 1)
            d_wmod[j % 2].up(sp.dma_start(wmod[j % 2][:], wmod_v[j]), 16)

        def load_wup(n):
            if n >= 2:
                pe_comb.wait(act, CH * (n - 1))
            d_wup[n % 2].up(act.dma_start(wup[n % 2][:], A["wup"][n]), 16)

        d_c.up(sp.dma_start(c_in[:], A["c"]), 16)
        load_wmod(0)
        load_wmod(1)
        d_ident.up(sp.dma_start(ident[:], A["ident"]), 16)
        d_wdk.up(act.dma_start(wdk[:], A["wdk"].rearrange("(c p) n -> p c n", p=P)), 16)
        load_wup(0)
        for b in range(BATCH):
            d_x[b].up((sp if b < 2 else act).dma_start(y[:, QT * b:QT * b + QT, :], x_tiles[b]), 16)
        load_wup(1)

        d_c.wait(act)
        act_pro.up(act.activation(c_exp[:], c_in[:], ACT.Exp, scale=-1.0))
        act_pro.wait(dve)
        n = dve_pro.up(dve.tensor_scalar(c_exp[:], c_exp[:], 1.0, None, ALU.add))
        dve_pro.wait(dve, n)
        n = dve_pro.up(dve.reciprocal(c_exp[:], c_exp[:]))
        dve_pro.wait(dve, n)
        silu_ready = dve_pro.up(dve.tensor_tensor(c_silu[:], c_in[:], c_exp[:], ALU.mult))
        dve_pro.up(dve.memset(power[:], -0.5))
        power_ready = dve_pro.value

        def modulation(j):
            ps = bank["ta" if j % 2 == 0 else "tb"]
            dve_pro.wait(pe, silu_ready)
            pe.wait_ge(d_wmod[j % 2].sem, 16 * (j // 2 + 1))
            if j >= 2:
                dve_mod.wait(pe, mod_read[j - 2])
            for c in range(CH):
                mm = pe.matmul(ps[0:BATCH, :], c_silu[:, c, :], wmod[j % 2][:, c, :], start=(c == 0), stop=(c == CH - 1))
            pe_mod.up(mm)
            pe_mod.wait(dve, j + 1)
            where = modrow[:, j, :] if j < 2 else modlate[:, j % 2, :]
            if j >= 4:
                dve.wait_ge(d_mod[j % 2].sem, 16)
            if j in (0, 3):
                mod_read.append(dve_mod.up(dve.tensor_copy(where, ps[0:BATCH, :])))
            elif j in (1, 4):
                mod_read.append(dve_mod.up(dve.tensor_scalar(where, ps[0:BATCH, :], 1.0, None, ALU.add)))
            else:
                if j == 5:
                    dve_mod.wait(dve, gate_read[0])
                dve_mod.up(dve.tensor_scalar(gate_a[:], ps[0:BATCH, :], 0.0, 2.0, ALU.is_ge, ALU.mult))
                dve_mod.wait(dve)
                mod_read.append(dve_mod.up(dve.scalar_tensor_tensor(
                    out=gate_b[:], in0=gate_a[:], scalar=-1.0, in1=ps[0:BATCH, :], op0=ALU.add, op1=ALU.mult)))
                dve_mod.wait(dve)
                dve_mod.up(dve.tensor_scalar(gate_b[:], gate_b[:], 0.25, None, ALU.max))
                dve_mod.wait(dve)
                gate_read.append(dve_mod.up(dve.scalar_tensor_tensor(
                    out=where, in0=gate_a[:], scalar=-1.0, in1=gate_b[:], op0=ALU.add, op1=ALU.mult)))
            if j >= 2:
                dve_mod.wait(sp)
                d_mod[j % 2].up(sp.dma_start(mod_d[j - 2], where), 16)

        mod_read, gate_read = [], []
        modulation(0)
        modulation(1)
        dve_mod.wait(pe)
        d_ident.wait(pe)
        for j in range(2):
            for c in range(CH):
                o = (j * CH + c) * BATCH
                mm = pe.transpose(bank["q"][:, o:o + BATCH], modrow[:, j, c * P:(c + 1) * P], ident[0:BATCH, 0:BATCH])
        pe_modT.up(mm)
        pe_modT.wait(dve)
        modT_ready = dve_pro.up(dve.tensor_copy(modT[:].rearrange("p j c b -> p (j c b)"),
                                                bank["q"][:, 0:2 * CH * BATCH]))
        load_wmod(2)
        load_wmod(3)
        for dst, name in ((cos_t, "cos"), (sin_t, "sin"), (mask, "mask")):
            d_const.up(sp.dma_start(dst[:], A[name]), 16)

        def layer_norm(b):
            d_x[b].wait(dve)
            for j in range(QT):
                if b or j:
                    pass
                m = dve.bn_stats(stats[:, j, :], y[:, QT * b + j, :])
            dve_ln.up(m)
            dve_ln.wait(dve)
            for j in range(QT):
                m = dve.bn_aggr(mean_var[:, QT * b + j, :], stats[:, j, :])
            dve_ln.up(m)
            dve_ln.wait(pool)
            dve_pro.wait(pool, power_ready)
            s = slice(QT * b, QT * b + QT)
            n = pool_ln.up(pool.tensor_scalar(ve[:, s], mean_var[:, s, 1], EPS, None, ALU.add))
            pool_ln.wait(pool, n)
            n = pool_ln.up(pool.tensor_tensor(rstd[:, s], ve[:, s], power[:, s], ALU.pow))
            pool_ln.wait(dve, n)
            for j in range(QT):
                i = QT * b + j
                m = dve.tensor_scalar(y[:, i, :], y[:, i, :], mean_var[:, i, 0:1], rstd[:, i:i + 1],
                                      ALU.subtract, ALU.mult)
            return dve_xn.up(m)

        def transpose_h(b, ready):
            for c in range(CH):
                n = b * CH + c
                ps = bank["s1" if n % 2 == 0 else "pv"]
                dve_xn.wait(pe, ready)
                if n >= 2:
                    dve_h.wait(pe, n - 1)
                for j in range(QT):
                    mm = pe.transpose(ps[:, j * P:(j + 1) * P], y[:, QT * b + j, c * P:(c + 1) * P], ident[:])
                pe_xt.up(mm)
                pe_xt.wait(dve, n + 1)
                if n == 0:
                    dve_pro.wait(dve, modT_ready)
                if n >= 2:
                    pool_h.wait(dve, n - 1)
                dve_h.up(dve.tensor_scalar(h_raw[n % 2][:], ps[:], modT[:, 1, c, b:b + 1], modT[:, 0, c, b:b + 1],
                                           ALU.mult, ALU.add))
                dve_h.wait(act, n + 1)
                act_h.up(act.activation(hT[0][:, n, :], h_raw[n % 2][:], ACT.Copy))
                act_h.wait(pool, n + 1)
                pool_h.up(pool.tensor_tensor(hT[1][:, n, :], h_raw[n % 2][:], hT[0][:, n, :].bitcast(F32),
                                             ALU.subtract))

        def combine(n):
            d_wdk.wait(pe, 16)
            pe.wait_ge(d_wup[n % 2].sem, 16 * (n // 2 + 1))
            for c in range(CH):
                i = n * CH + c
                ps = bank["s3" if i % 2 == 0 else "s2"]
                if i >= 2:
                    act_comb.wait(pe, i - 1)
                for m in range(CH):
                    mm = pe.matmul(ps[:, 0:2 * KVC], wdk[:, m, c * P:(c + 1) * P], wup[n % 2][:, m, :],
                                   start=(m == 0), stop=(m == CH - 1))
                pe_comb.up(mm)
                pe_comb.wait(act, i + 1)
                if i >= 4:
                    act.wait_ge(d_wc[i % 4].sem, 16 * (i // 4))
                act_comb.up(act.activation(wc_out[i % 4][:], ps[:, 0:2 * KVC], ACT.Copy))
                act_comb.wait(sp, i + 1)
                d_wc[i % 4].up(sp.dma_start(wc_d[2 * n:2 * n + 2, :, c, :].rearrange("g p k -> p g k"),
                                            wc_out[i % 4][:].rearrange("p (g k) -> p g k", g=2)), 16)

        act_w = mark("act_w", 1, len(CHUNKS))
        pool_w = mark("pool_w", 1, len(CHUNKS))
        d_w = [ctx.enter_context(nc.semaphore(f"d_w{i}")) for i in range(2)]
        parts = [2 if c == "wk" else 1 for c in CHUNKS]
        FIRST = len(FIRST_CHUNKS)

        def chunk_event(i):
            return FIRST + i

        def dma_value(g, i):
            per = sum(parts[j] for j in range(i % 2, len(CHUNKS), 2))
            before = sum(parts[4 + j] for j in range(i % 2, FIRST, 2))
            local = sum(parts[j] for j in range(i % 2, i + 1, 2))
            return g * (16 * per) + 16 * (before + local)

        def first_dma_value(i):
            return 16 * sum(parts[4 + j] for j in range(i % 2, i + 1, 2))

        def chunk_load(g, name, slot, free):
            free()
            to = stage[slot]
            if name.startswith("wo"):
                src = A["wo"][bass.ts(g * GROUP + int(name[2]), P), :]
                sp.dma_start(to[:], src).then_inc(d_w[slot], 16)
            elif name.startswith("wq"):
                src = A["wq"][bass.ts(g * GROUP + int(name[2]), P), :]
                sp.dma_start(to[:], src).then_inc(d_w[slot], 16)
            elif name == "wv":
                src = wc_rows[bass.ts(g, P), :].rearrange("p (c k) -> p c k", c=CH)[:, :, NOPE:KVC]
                sp.dma_start(to[:].rearrange("p (c k) -> p c k", c=CH), src).then_inc(d_w[slot], 16)
            else:
                cols = to[:].rearrange("p (a k) -> p a k", k=2 * ROPE_HALF)
                rope = A["wkr"][bass.ts(g, P), :].rearrange("p (a k) -> p a k", k=ROPE_HALF)
                sp.dma_start(cols[:, :, 0:ROPE_HALF], rope).then_inc(d_w[slot], 16)
                nope = wc_rows[bass.ts(g, P), :].rearrange("p (c k) -> p c k", c=CH)[:, :, 0:NOPE]
                for_c = to[:].rearrange("p (c a k) -> p c a k", c=CH, a=2)[:, :, :, ROPE_HALF:2 * ROPE_HALF]
                sp.dma_start(for_c, nope.rearrange("p c (a k) -> p c a k", a=2)).then_inc(d_w[slot], 16)

        wc_rows = wc_d.rearrange("g p c k -> (g p) (c k)")

        def chunk_target(name):
            n = int(name[2]) if name[-1].isdigit() else 0
            flat = {"wo": lambda w: wo[w][:, n, :],
                    "wq": lambda w: wq[w][:, n].rearrange("p c d -> p (c d)"),
                    "wk": lambda w: wk[w][:].rearrange("p c d -> p (c d)"),
                    "wv": lambda w: wv[w][:].rearrange("p c d -> p (c d)")}[name[:2]]
            return flat(0), flat(1)

        def chunk_split(name, slot, landed, event, free):
            hi, lo = chunk_target(name)
            act.wait_ge(d_w[slot], landed)
            free()
            act_w.up(act.activation(hi, stage[slot][:], ACT.Copy))
            act_w.wait(pool, event)
            pool_w.up(pool.tensor_tensor(lo, stage[slot][:], hi.bitcast(F32), ALU.subtract))

        pe_t = mark("pe_t", 3)
        pe_s = mark("pe_s", 4)
        pe_qp = mark("pe_qp")
        pe_pv = mark("pe_pv")
        pe_v = mark("pe_v", 1, BATCH)
        pe_k = mark("pe_k", 1, BATCH)
        pe_vt = mark("pe_vt", 1, BATCH)
        pe_op = mark("pe_op", QT, BATCH)
        act_t = mark("act_t", 3)
        act_exp = mark("act_exp", 2)
        act_norm = mark("act_norm")
        act_q = mark("act_q")
        act_o = mark("act_o")
        act_vraw = mark("act_vraw", 1, BATCH)
        act_v = mark("act_v", 1, BATCH)
        act_kn = mark("act_kn", 1, BATCH)
        act_k = mark("act_k", 1, BATCH)
        dve_t = mark("dve_t", 3)
        dve_s = mark("dve_s", 2)
        dve_nm = mark("dve_nm", 2)
        dve_ri = mark("dve_ri", 2)
        dve_r = mark("dve_r")
        dve_o = mark("dve_o")
        dve_v = mark("dve_v", 1, BATCH)
        dve_kr = mark("dve_kr", 1, BATCH)
        dve_y = mark("dve_y", QT, BATCH, start=1)
        pool_a = mark("pool_a")
        pool_q = mark("pool_q")
        pool_ka = mark("pool_ka", 1, BATCH)
        pool_k = mark("pool_k", 1, BATCH)

        def passes(hi_lo_a, hi_lo_b):
            return [(hi_lo_a[0], hi_lo_b[1]), (hi_lo_a[1], hi_lo_b[0]), (hi_lo_a[0], hi_lo_b[0])]

        def unit_of(t):
            return t[0], t[1] // GROUP

        def before(t, n=1):
            return t[0], t[1] - n

        def q_proj(t):
            g, k = t
            b, h = (k // GROUP) % BATCH, k % GROUP
            dve_r.wait(pe, before(t))
            if b == 0:
                i = CHUNKS.index(f"wq{h}")
                shift = 0 if k < STEPS else 1
                pool_w.wait(pe, (g, len(CHUNKS) * (shift - 1) + chunk_event(i)), 1)
            for c in range(CH):
                for n, (w, x) in enumerate(passes(wq, hT)):
                    mm = pe.matmul(bank["q"][:], w[:, h, c, :], x[:, b * CH + c, :],
                                   start=(c == 0 and n == 0), stop=(c == CH - 1 and n == 2))
            pe_qp.up(mm)

        def q_rope(t, k_first=False):
            pe_qp.wait(dve, t)
            pool_q.wait(dve, before(t))
            if t[1] % GROUP == 1 or k_first:
                pool_ka.wait(dve, unit_of(t))
            dve.tensor_tensor(rot_c[:], bank["q"][:], cos_t[:], ALU.mult)
            dve.tensor_tensor(rot_s[0:64, :], bank["q"][64:128, :], sin_t[64:128, :], ALU.mult)
            dve_r.up(dve.tensor_tensor(rot_s[64:128, :], bank["q"][0:64, :], sin_t[0:64, :], ALU.mult))
            dve_r.wait(pool, t)
            pool_a.up(pool.tensor_tensor(rot_c[:], rot_c[:], rot_s[:], ALU.add))

        def q_split(t):
            hi, lo = qT[t[1] % 2]
            pool_a.wait(act, t)
            pe_s.wait(act, before(t, 2))
            act_q.up(act.activation(hi[:], rot_c[:], ACT.Copy))
            act_q.wait(pool, t)
            pool_q.up(pool.tensor_tensor(lo[:], rot_c[:], hi[:].bitcast(F32), ALU.subtract))

        def project(u, weights, chunk):
            g, b = u
            if b % BATCH == 0:
                shift = 0 if b < BATCH else 1
                pool_w.wait(pe, (g, len(CHUNKS) * (shift - 1) + chunk_event(CHUNKS.index(chunk))), 1)
            for c in range(CH):
                for n, (w, x) in enumerate(passes(weights, hT)):
                    mm = pe.matmul(bank["x"][:], w[:, c, :], x[:, (b % BATCH) * CH + c, :],
                                   start=(c == 0 and n == 0), stop=(c == CH - 1 and n == 2))
            return mm

        def k_proj(u):
            dve_y.wait(pe, before(u, 2))
            pe_k.up(project(u, wk, "wk"))

        def v_proj(u):
            act_kn.wait(pe, u)
            pe_v.up(project(u, wv, "wv"))

        def v_raw(u):
            pe_v.wait(act, u)
            act_k.wait(act, u)
            pool_k.wait(act, u)
            act_vraw.up(act.activation(kv_raw[:], bank["x"][:], ACT.Copy))

        def k_rope(u, last_q):
            ps = bank["x"]
            pe_k.wait(dve, u)
            pool_a.wait(dve, last_q)
            dve.tensor_tensor(kv_raw[:], ps[:], cos_t[:], ALU.mult)
            dve.tensor_tensor(rot_s[0:32, :], ps[64:96, :], sin_t[64:96, :], ALU.mult)
            dve_kr.up(dve.tensor_tensor(rot_s[64:96, :], ps[0:32, :], sin_t[0:32, :], ALU.mult))
            dve_kr.wait(pool, u)
            pool_ka.up(pool.tensor_tensor(kv_raw[:], kv_raw[:], rot_s[:], ALU.add))

        def k_nope(u):
            pool_ka.wait(act, u)
            act.activation(kv_raw[32:64, :], bank["x"][32:64, :], ACT.Copy)
            act_kn.up(act.activation(kv_raw[96:128, :], bank["x"][96:128, :], ACT.Copy))

        def k_split(u):
            act_kn.wait(act, u)
            pe_s.wait(act, (u[0], GROUP * u[1] - 1))
            act_k.up(act.activation(kT[0][:], kv_raw[:], ACT.Copy))
            act_k.wait(pool, u)
            pool_k.up(pool.tensor_tensor(kT[1][:], kv_raw[:], kT[0][:].bitcast(F32), ALU.subtract))

        def v_transpose(u):
            act_vraw.wait(pe, u)
            for j in range(QT):
                mm = pe.transpose(bank["x"][:, j * P:(j + 1) * P], kv_raw[:, j * P:(j + 1) * P], ident[:])
            pe_vt.up(mm)

        v_flat = [w[:].rearrange("p j d -> p (j d)") for w in v]

        def v_split_hi(u):
            pe_vt.wait(act, u)
            pe_pv.wait(act, (u[0], GROUP * u[1] - 1))
            act_v.up(act.activation(v_flat[0], bank["x"][:], ACT.Copy))

        def v_split_lo(u):
            act_v.wait(dve, u)
            dve_v.up(dve.tensor_tensor(v_flat[1], bank["x"][:], v_flat[0].bitcast(F32), ALU.subtract))

        score_bank = {3: bank["s3"][:, 0:512], 2: bank["s2"][:, 0:384], 1: bank["s1"][:, 0:256],
                      0: bank["s1"][:, 256:384]}
        QUERY_ORDER = [3, 2, 1, 0]

        def scores(t):
            pool_q.wait(pe, t)
            if t[1] % GROUP == 0:
                pool_k.wait(pe, unit_of(t))
            dve_s.wait(pe, before(t))
            for qt in QUERY_ORDER:
                for n, (q, k) in enumerate(passes(qT[t[1] % 2], kT)):
                    mm = pe.matmul(score_bank[qt], q[:, qt * P:(qt + 1) * P], k[:, 0:(qt + 1) * P],
                                   start=(n == 0), stop=(n == 2))
                pe_s.up(mm)

        def row(t, qt):
            return probs[t[1] % 2][:, q_offset(qt):q_offset(qt + 1)]

        def mask_and_max(t, half):
            m = t[1] % 2
            for qt in HALVES[half]:
                if qt:
                    pe_s.wait(dve, t, 4 if qt == 1 else 4 - qt)
                    dve.memset(wait_slot[:, qt:qt + 1], 0.0)
                ins = dve.tensor_tensor_reduce(row(t, qt), score_bank[qt], mask[:, SEQ - (qt + 1) * P:], 1.0, LOWEST,
                                               ALU.add, ALU.max, row_max[m][:, qt:qt + 1])
            dve_s.up(ins)
            dve_s.wait(dve, t, half + 1)
            cols = slice(HALVES[half][1], HALVES[half][0] + 1)
            dve_nm.up(dve.tensor_scalar(neg_max[m][:, cols], row_max[m][:, cols], -SCALE, None, ALU.mult))

        def exponentials(t, half):
            m = t[1] % 2
            dve_nm.wait(act, t, half + 1)
            for qt in HALVES[half]:
                ins = act.activation(row(t, qt), row(t, qt), ACT.Exp, bias=neg_max[m][:, qt:qt + 1], scale=SCALE,
                                     accum_out=row_sum[m][:, qt:qt + 1])
            act_exp.up(ins)

        def invert_sums(t, half):
            m = t[1] % 2
            cols = slice(HALVES[half][1], HALVES[half][0] + 1)
            act_exp.wait(dve, t, half + 1)
            dve_ri.up(dve.reciprocal(row_inv[m][:, cols], row_sum[m][:, cols]))

        def normalise(t, half):
            dve_ri.wait(act, t, half + 1)
            for qt in HALVES[half]:
                ins = act.activation(row(t, qt), row(t, qt), ACT.Copy, scale=row_inv[t[1] % 2][:, qt:qt + 1])
            if half:
                act_norm.up(ins)

        T_PARTS = [("ta", [0]), ("tb", [1, 3]), ("ta", [2])]

        def transpose_part(t, n):
            name, keys = T_PARTS[n]
            start = KEY_OFFSET[keys[0]]
            if n == 0:
                act_norm.wait(pe, t)
                dve_t.wait(pe, before(t))
            if n == 2:
                dve_t.wait(pe, t, 1)
            for kb in keys:
                for qt in range(kb, QT):
                    o = KEY_OFFSET[kb] - start + (qt - kb) * P
                    mm = pe.transpose(bank[name][:, o:o + P], row(t, qt)[:, kb * P:(kb + 1) * P], ident[:])
            pe_t.up(mm)

        def part_range(n):
            keys = T_PARTS[n][1]
            start = KEY_OFFSET[keys[0]]
            return start, sum((QT - kb) * P for kb in keys)

        def split_part(t, n):
            at, size = part_range(n)
            pe_t.wait(act, t, n + 1)
            act_t.up(act.activation(PT[0][:, at:at + size], bank[T_PARTS[n][0]][:, 0:size], ACT.Copy))

            act_t.wait(dve, t, n + 1)
            dve_t.up(dve.tensor_tensor(PT[1][:, at:at + size], bank[T_PARTS[n][0]][:, 0:size],
                                       PT[0][:, at:at + size].bitcast(F32), ALU.subtract))

        def values(t, first_unit=False):
            h = t[1] % GROUP
            dve_t.wait(pe, t)
            if h == 0:
                dve_v.wait(pe, unit_of(t))
                dve_y.wait(pe, before(unit_of(t)), 3)
            else:
                dve_o.wait(pe, before(t))
            for kb in KEY_ORDER:
                for n, (a, p) in enumerate(passes(v, PT)):
                    mm = pe.matmul(bank["pv"][:, kb * P:SEQ], a[:, kb, :],
                                   p[:, KEY_OFFSET[kb]:KEY_OFFSET[kb] + (QT - kb) * P],
                                   start=(kb == 0 and n == 0), stop=(kb == KEY_ORDER[-1] and n == 2))
            pe_pv.up(mm)

        def o_split_hi(t):
            pe_pv.wait(act, t)
            act_o.up(act.activation(OT[0][:, t[1] % GROUP, :], bank["pv"][:], ACT.Copy))

        def o_split_lo(t):
            h = t[1] % GROUP
            act_o.wait(dve, t)
            dve_o.up(dve.tensor_tensor(OT[1][:, h, :], bank["pv"][:], OT[0][:, h, :].bitcast(F32), ALU.subtract))

        def out_proj(u, last=False):
            dve_o.wait(pe, (u[0], GROUP * u[1] + GROUP - 1))
            if u[1] == 0:
                pool_w.wait(pe, (u[0], chunk_event(3)), 1)
            for j in range(QT):
                ps = bank["pv" if j % 2 == 0 else "x"]
                if j == 1 and not last:
                    dve_v.wait(pe, (u[0], u[1] + 1))
                if j >= 2:
                    dve_y.wait(pe, u, j - 1)
                for h in range(GROUP):
                    for n, (o, w) in enumerate(passes(OT, wo)):
                        mm = pe.matmul(ps[:], o[:, h, j * P:(j + 1) * P], w[:, h, :],
                                       start=(h == 0 and n == 0), stop=(h == GROUP - 1 and n == 2))
                pe_op.up(mm)

        def add_out(u):
            for j in range(QT):
                ps = bank["pv" if j % 2 == 0 else "x"]
                i = (u[1] % BATCH) * QT + j
                pe_op.wait(dve, u, j + 1)
                dve_y.up(dve.tensor_tensor(y[:, i, :], ps[:], y[:, i, :], ALU.add))

        def step(g, k, last=False, first=False):
            t, u = (g, k), (g, k // GROUP)
            h = k % GROUP
            has1, has3 = not last or k + 1 < STEPS, not last or k + 3 < STEPS
            more = not last or u[1] + 1 < BATCH
            nxt1, nxt3, prev, un = (g, k + 1), (g, k + 3), (g, k - 1), (g, u[1] + 1)
            nxt2 = (g, k + 2)
            has2 = not last or k + 2 < STEPS

            transpose_part(t, 0)
            transpose_part(t, 1)
            if has1:
                scores(nxt1)
            transpose_part(t, 2)
            if has3:
                q_proj(nxt3)
            if h == 0 and not first:
                out_proj(before(u))
            if more and h == 1:
                k_proj(un)
            if more and h == 2:
                v_proj(un)
            if more and h == 3:
                v_transpose(un)
            values(t)

            split_part(t, 0)
            split_part(t, 1)
            if not first:
                o_split_hi(prev)
            if h == 0:
                v_split_hi(u)
            if more and h == 2:
                k_nope(un)
            if more and h == 3:
                v_raw(un)
            if has2 and not first:
                q_split(nxt2)
            if more and h == 2:
                k_split(un)
            split_chunks(g, k, last)
            if has1:
                mask_and_max(nxt1, 0)
                exponentials(nxt1, 0)
                mask_and_max(nxt1, 1)
            split_part(t, 2)
            if not first:
                o_split_lo(prev)
            if h == 0:
                v_split_lo(u)
            if has1:
                exponentials(nxt1, 1)
                for half in (0, 1):
                    invert_sums(nxt1, half)
                    normalise(nxt1, half)
            if has3:
                q_rope(nxt3)
            if more and h == 1:
                k_rope(un, nxt3)
            if h == 0 and not first:
                add_out(before(u))

        def split_chunks(g, k, last):
            for i in CHUNK_STEP.get(k, []):
                name = CHUNKS[i]
                if last and i >= 4:
                    continue

                def free(name=name):
                    if name[:2] == "wo":
                        pe_pv.wait(act, (g, 0))
                    elif name == "wv":
                        pe_v.wait(act, (g, BATCH - 1))
                    elif name == "wk":
                        pe_k.wait(act, (g, BATCH - 1))
                    else:
                        pe_qp.wait(act, (g, STEPS - GROUP + int(name[2])))
                chunk_split(name, i % 2, dma_value(g, i), (g, chunk_event(i)), free)

        def group_loads(g, last=False):
            for i, name in enumerate(CHUNKS):
                if last and i >= 4:
                    break

                def stage_free(i=i):
                    pool_w.wait(sp, (g, chunk_event(i) - 2), 1)
                chunk_load(g if i < 4 else g + 1, name, i % 2, stage_free)

        ready = [layer_norm(0)]
        transpose_h(0, ready[0])
        combine(0)
        for b in range(1, BATCH):
            ready.append(layer_norm(b))
            transpose_h(b, ready[b])
            if b + 1 < BATCH:
                load_wup(b + 1)
            combine(b)
            modulation(b + 1)
            if b + 3 < 6:
                load_wmod(b + 3)
        modulation(5)
        pe_xt.wait(pool)
        dve_y.up(pool.memset(y[:], 0.0))

        for w in d_wc:
            w.wait(sp)
        for i, name in enumerate(FIRST_CHUNKS):
            def stage_free(i=i):
                if i >= 2:
                    pool_w.wait(sp, (0, i - 2), 1)
            chunk_load(0, name, i % 2, stage_free)
            chunk_split(name, i % 2, first_dma_value(i), (0, i), lambda: None)
        for e in (pe, act, dve, pool):
            pe_comb.wait(e)
            pe_mod.wait(e)
            pool_h.wait(e)
            act_comb.wait(e)
            for w in d_mod + d_wc:
                w.wait(e)
        rot_clear = dve_pro.up(dve.memset(rot_s[:], 0.0))
        dve_pro.wait(dve, rot_clear)
        d_const.wait(dve)
        dve_y.wait(dve, (0, -1))

        zero = (0, 0)
        k_proj(zero)
        k_rope(zero, (0, -1))
        k_nope(zero)
        k_split(zero)
        v_proj(zero)
        v_raw(zero)
        v_transpose(zero)
        q_proj(zero)
        q_rope(zero, k_first=True)
        q_split(zero)
        scores(zero)
        for half in (0, 1):
            mask_and_max(zero, half)
            exponentials(zero, half)
        for half in (0, 1):
            invert_sums(zero, half)
            normalise(zero, half)
        for n in (1, 2):
            q_proj((0, n))
            q_rope((0, n))
            q_split((0, n))
        step(0, 0, first=True)

        with nc.Fori(0, KV - 1) as g:
            group_loads(g)
            for k in range(1, STEPS + 1):
                step(g, k)
        group_loads(KV - 1, last=True)
        for k in range(1, STEPS):
            step(KV - 1, k, last=True)
        final = (KV - 1, STEPS - 1)
        o_split_hi(final)
        o_split_lo(final)
        out_proj((KV - 1, BATCH - 1), last=True)
        add_out((KV - 1, BATCH - 1))

        ffn = Region(attention_only)
        gate1, shift2, scale2, gate2 = (
            [ffn.take(f"{n}{b}", [P, HID]) for b in range(BATCH)] for n in ("gate1_", "shift2_", "scale2_", "gate2_"))
        experts = ffn.take("experts", [EXPERTS, HID])
        router = ffn.take("router", [P, CH, EXPERTS])
        router_bias = ffn.take("router_bias", [P, EXPERTS])
        NB = 3
        x_in = [ffn.take(f"x_in{i}", [P, HID]) for i in range(NB)]
        h2 = [ffn.take(f"h2_{i}", [P, HID]) for i in range(NB)]
        h2T = [ffn.take(f"h2T_{i}", [P, CH, P]) for i in range(NB)]
        res = [ffn.take(f"res{i}", [P, HID]) for i in range(NB)]
        bn6 = [ffn.take(f"bn6_{i}", [P, 8]) for i in range(NB)]
        small = [ffn.take(f"small{i}", [P, 16]) for i in range(NB)]
        top8 = [ffn.take(f"top8_{i}", [P, 8]) for i in range(NB)]
        logit = [ffn.take(f"logit{i}", [P, EXPERTS]) for i in range(NB)]
        rest = [ffn.take(f"rest{i}", [P, EXPERTS]) for i in range(NB)]
        weight = [ffn.take(f"weight{i}", [P, EXPERTS]) for i in range(NB)]
        weightT = [ffn.take(f"weightT{i}", [EXPERTS, P]) for i in range(NB)]
        half = ffn.take("half", [P, 1])
        assert ffn.at <= nc.sbuf_usable_end

        d_ffn, d_xin, d_out = count("d_ffn"), [count(f"d_xin{i}") for i in range(NB)], [count(f"d_out{i}") for i in range(NB)]
        f = {n: count(f"f_{n}") for n in ("dve", "pool", "act", "pe")}
        dve_y.wait(sp, (KV - 1, BATCH - 1))
        pool_w.wait(sp, (KV - 1, chunk_event(3)), 1)
        for n, tiles in enumerate((gate1, shift2, scale2, gate2)):
            for b in range(BATCH):
                d_ffn.up(sp.dma_start(tiles[b][:], mod_d[n, b:b + 1, :].broadcast_to([P, HID])), 16)
        d_ffn.up(sp.dma_start(experts[:], A["eb"]), 16)
        d_ffn.up(sp.dma_start(router[:], A["rw"]), 16)
        d_ffn.up(sp.dma_start(router_bias[:], A["rb"].broadcast_to([P, EXPERTS])), 16)
        dve_y.wait(dve, (KV - 1, BATCH - 1))
        f["dve"].up(dve.memset(half[:], -0.5))
        for e in (dve, pool, pe, act):
            dve_y.wait(e, (KV - 1, BATCH - 1))
            d_ffn.wait(e)

        def self_wait(engine, name):
            f[name].wait(engine)

        x_rows = A["x"].rearrange("(i p) n -> i p n", p=P)
        out_rows = out.rearrange("(i p) n -> i p n", p=P)
        done = {}

        def load_x(i):
            if i >= NB:
                sp.wait_ge(f["dve"].sem, done[("x1", i - NB)])
            d_xin[i % NB].up(sp.dma_start(x_in[i % NB][:], x_rows[i]), 16)

        def ffn_norm(i):
            b, m = i // QT, i % NB
            load_x(i)
            yi, s = y[:, i, :], small[m]
            f["dve"].up(dve.tensor_tensor(yi, yi, gate1[b][:], ALU.mult))
            self_wait(dve, "dve")
            d_xin[m].wait(dve)
            done[("x1", i)] = f["dve"].up(dve.tensor_tensor(yi, yi, x_in[m][:], ALU.add))
            self_wait(dve, "dve")
            if i >= NB:
                dve.wait_ge(f["dve"].sem, done[("out", i - NB)])
            f["dve"].up(dve.bn_stats(bn6[m][:, 0:6], yi))
            self_wait(dve, "dve")
            f["dve"].up(dve.bn_aggr(s[:, 0:2], bn6[m][:, 0:6]))
            f["dve"].wait(pool)
            f["pool"].up(pool.tensor_scalar(s[:, 2:3], s[:, 1:2], EPS, None, ALU.add))
            self_wait(pool, "pool")
            f["pool"].up(pool.tensor_tensor(s[:, 3:4], s[:, 2:3], half[:], ALU.pow))
            f["pool"].wait(dve)
            if i >= NB:
                dve.wait_ge(f["pe"].sem, done[("h2T", i - NB)])
            f["dve"].up(dve.tensor_scalar(h2[m][:], yi, s[:, 0:1], s[:, 3:4], ALU.subtract, ALU.mult))
            f["dve"].wait(pool)
            f["pool"].up(pool.tensor_tensor(h2[m][:], h2[m][:], scale2[b][:], ALU.mult))
            self_wait(pool, "pool")
            done[("h2", i)] = f["pool"].up(pool.tensor_tensor(h2[m][:], h2[m][:], shift2[b][:], ALU.add))

        def ffn_router(i):
            m = i % NB
            ps, pl = bank["ta" if i % 2 == 0 else "tb"], bank["s3" if i % 2 == 0 else "s2"]
            pe.wait_ge(f["pool"].sem, done[("h2", i)])
            if i >= 2:
                pe.wait_ge(f["act"].sem, done[("h2T_copy", i - 2)])
                pe.wait_ge(f["dve"].sem, done[("logit", i - 2)])
            for c in range(CH):
                mm = pe.transpose(ps[:, c * P:(c + 1) * P], h2[m][:, c * P:(c + 1) * P], ident[:])
            done[("h2T", i)] = f["pe"].up(mm)
            f["pe"].wait(act)
            done[("h2T_copy", i)] = f["act"].up(act.activation(h2T[m][:].rearrange("p c t -> p (c t)"), ps[:], ACT.Copy))
            f["act"].wait(pe)
            for c in range(CH):
                mm = pe.matmul(pl[:, 0:EXPERTS], h2T[m][:, c, :], router[:, c, :], start=(c == 0), stop=(c == CH - 1))
            done[("logits_mm", i)] = f["pe"].up(mm)
            f["pe"].wait(dve)
            s = small[m]
            done[("logit", i)] = f["dve"].up(dve.tensor_tensor_reduce(
                logit[m][:], pl[:, 0:EXPERTS], router_bias[:], 1.0, LOWEST, ALU.add, ALU.max, s[:, 4:5]))
            self_wait(dve, "dve")
            f["dve"].up(dve.tensor_scalar(s[:, 5:6], s[:, 4:5], -1.0, None, ALU.mult))
            f["dve"].wait(act)
            f["act"].up(act.activation(logit[m][:], logit[m][:], ACT.Exp, bias=s[:, 5:6], accum_out=s[:, 6:7]))
            f["act"].wait(dve)
            f["dve"].up(dve.reciprocal(s[:, 7:8], s[:, 6:7]))
            f["dve"].up(dve.max(top8[m][:], logit[m][:]))
            self_wait(dve, "dve")
            f["dve"].up(dve.match_replace(rest[m][:], top8[m][:], logit[m][:], 0.0))
            self_wait(dve, "dve")
            f["dve"].up(dve.tensor_tensor(rest[m][:], logit[m][:], rest[m][:], ALU.subtract))
            self_wait(dve, "dve")
            if i >= NB:
                dve.wait_ge(f["pe"].sem, done[("mix", i - NB)])
            done[("weight", i)] = f["dve"].up(dve.tensor_scalar(
                weight[m][:], rest[m][:], s[:, 7:8], 0.0, ALU.mult, ALU.add, accum_out=s[:, 8:9]))

        def ffn_mix(i):
            b, m = i // QT, i % NB
            pw, px = bank["s1" if i % 2 == 0 else "q"], bank["pv" if i % 2 == 0 else "x"]
            pe.wait_ge(f["dve"].sem, done[("weight", i)])
            if i >= 2:
                pe.wait_ge(f["act"].sem, done[("wT", i - 2)])
                pe.wait_ge(f["dve"].sem, done[("mixed", i - 2)])
            f["pe"].up(pe.transpose(pw[0:EXPERTS, 0:P], weight[m][:], ident[:]))
            f["pe"].wait(act)
            done[("wT", i)] = f["act"].up(act.activation(weightT[m][:], pw[0:EXPERTS, 0:P], ACT.Copy))
            f["act"].wait(pe)
            done[("mix", i)] = f["pe"].up(pe.matmul(px[:], weightT[m][:], experts[:], start=True, stop=True))
            f["pe"].wait(dve)
            s = small[m]
            dve.wait_ge(f["pool"].sem, done[("h2", i)])
            if i >= NB:
                d_out[m].wait(dve)
            done[("mixed", i)] = f["dve"].up(dve.scalar_tensor_tensor(
                out=res[m][:], in0=h2[m][:], scalar=s[:, 8:9], in1=px[:], op0=ALU.mult, op1=ALU.add))
            f["dve"].wait(pool)
            f["pool"].up(pool.tensor_tensor(res[m][:], res[m][:], gate2[b][:], ALU.mult))
            f["pool"].wait(dve)
            done[("out", i)] = f["dve"].up(dve.tensor_tensor(res[m][:], res[m][:], y[:, i, :], ALU.add))
            f["dve"].wait(sp)
            d_out[m].up(sp.dma_start(out_rows[i], res[m][:]), 16)

        for i in range(TILES + 2):
            if i < TILES:
                ffn_norm(i)
            if 1 <= i <= TILES:
                ffn_router(i - 1)
            if i >= 2:
                ffn_mix(i - 2)
        for w in d_out:
            w.wait(sp)


def kernel(L0_attn_hidden_states, L0_attn_Wq, L0_attn_Wkr, L0_attn_Wdk, L0_attn_Wupk, L0_attn_Wupv, L0_attn_Wo,
           L0_ffn_router_weight, L0_ffn_router_bias, L0_ffn_expert_bias, L0_c, L0_wmod):
    import concourse.bacc as bacc
    from concourse.bass_utils import run_bass_kernel_spmd

    def lay(a, shape=None):
        a = np.ascontiguousarray(a)
        return a if shape is None else a.reshape(shape)

    upk = np.asarray(L0_attn_Wupk).reshape(KV, NOPE, HID)
    upv = np.asarray(L0_attn_Wupv).reshape(KV, HD, HID)
    up = np.concatenate([upk, upv], axis=1).reshape(KV // 2, 2 * KVC, CH, P).transpose(0, 3, 2, 1)
    inv_freq = 1.0 / 10000.0 ** (np.arange(0, HD, 2, dtype=np.float32) / HD)
    freqs = np.outer(np.arange(SEQ, dtype=np.float32), inv_freq)
    emb = np.concatenate([freqs, freqs], axis=-1)
    sign = np.concatenate([np.ones(HD // 2, np.float32), -np.ones(HD // 2, np.float32)])[:, None]
    causal = np.zeros((P, SEQ), np.float32)
    causal[:, SEQ - P:] = np.where(np.tril(np.ones((P, P), bool)), 0.0, MASKED)
    arrays = {
        "x": lay(L0_attn_hidden_states, (BATCH * SEQ, HID)),
        "c": lay(np.asarray(L0_c).T.reshape(CH, P, BATCH).transpose(1, 0, 2)),
        "wmod": lay(L0_wmod),
        "wq": lay(np.asarray(L0_attn_Wq).reshape(HEADS, HD, CH, P).transpose(0, 3, 2, 1), (HEADS * P, HID)),
        "wkr": lay(np.asarray(L0_attn_Wkr).reshape(KV, 2 * ROPE_HALF, CH, P).transpose(0, 3, 2, 1),
                   (KV * P, CH * 2 * ROPE_HALF)),
        "wdk": lay(L0_attn_Wdk),
        "wup": lay(up),
        "wo": lay(np.asarray(L0_attn_Wo).T),
        "rw": lay(np.asarray(L0_ffn_router_weight).T.reshape(CH, P, EXPERTS).transpose(1, 0, 2)),
        "rb": lay(L0_ffn_router_bias, (1, EXPERTS)),
        "eb": lay(L0_ffn_expert_bias),
        "cos": lay(np.cos(emb).astype(np.float32).T),
        "sin": lay(np.sin(emb).astype(np.float32).T * sign),
        "mask": causal,
        "ident": np.eye(P, dtype=np.float32),
    }
    nc = bacc.Bacc("TRN2", target_bir_lowering=False, num_devices=1)
    aps = {n: nc.dram_tensor(f"in_{n}", a.shape, F32, kind="ExternalInput").ap() for n, a in arrays.items()}
    out = nc.dram_tensor("out_y", (BATCH * SEQ, HID), F32, kind="ExternalOutput").ap()
    build(nc, aps, out)
    r = run_bass_kernel_spmd(nc, [{f"in_{n}": a for n, a in arrays.items()}], core_ids=[0])
    return r.results[0]["out_y"].reshape(BATCH, SEQ, HID)
```

```python
from contextlib import ExitStack

import numpy as np

import concourse.bass as bass
from concourse import mybir

F32 = mybir.dt.float32
F32R = mybir.dt.float32r
ALU = mybir.AluOpType
ACT = mybir.ActivationFunctionType

P = 128
BATCH, SEQ, HID = 4, 512, 512
HEADS, KV, HD = 32, 8, 128
GROUP = HEADS // KV
LOW = 64
ROPE_HALF = 32
EXPERTS = 64
CH = HID // P
QT = SEQ // P
TILES = BATCH * QT
STEPS = BATCH * GROUP
NOPE = HD - 2 * ROPE_HALF
KVC = NOPE + HD
CAUSAL = P * QT * (QT + 1) // 2
SCALE = 1.0 / float(np.sqrt(np.float32(HD)))
EPS = 1e-5
MASKED = -1e30
LOWEST = -3e38

CHUNKS = ["wo0", "wo1", "wo2", "wo3", "wk", "wq0", "wv", "wq1", "wq2", "wq3"]
CHUNK_STEP = {1: [0, 1], 2: [2], 3: [3], 10: [4, 5], 11: [6], 12: [7], 13: [8], 14: [9]}
HALVES = [(3, 2), (1, 0)]
FIRST_CHUNKS = CHUNKS[4:]


def q_offset(qt):
    return P * qt * (qt + 1) // 2


KEY_ORDER = [0, 1, 3, 2]
KEY_OFFSET = {0: 0, 1: 512, 3: 896, 2: 1024}


class Mark:

    def __init__(self, ctx, nc, name, per=1, stride=STEPS, start=0):
        self.sem, self.per, self.stride, self.start = ctx.enter_context(nc.semaphore(name)), per, stride, start

    def up(self, instruction):
        instruction.then_inc(self.sem, 1)

    def wait(self, engine, t, n=None):
        g, k = t
        n = self.per if n is None else n
        constant = self.start + self.per * k + n
        if isinstance(g, int):
            value = self.per * self.stride * g + constant
            if value > 0:
                engine.wait_ge(self.sem, value)
        else:
            assert constant > 0
            engine.wait_ge(self.sem, g * (self.per * self.stride) + constant)


class Count:

    def __init__(self, ctx, nc, name):
        self.sem, self.value = ctx.enter_context(nc.semaphore(name)), 0

    def up(self, instruction, by=1):
        instruction.then_inc(self.sem, by)
        self.value += by
        return self.value

    def wait(self, engine, value=None):
        engine.wait_ge(self.sem, self.value if value is None else value)


def build(nc, A, out):
    pe, act, dve, pool, sp = nc.tensor, nc.scalar, nc.vector, nc.gpsimd, nc.sync
    ctx = ExitStack()
    with ctx:
        def mark(name, per=1, stride=STEPS, start=0):
            return Mark(ctx, nc, name, per, stride, start)

        def count(name):
            return Count(ctx, nc, name)

        F_RING, W_RING = 5, 4
        base = (nc.sbuf_base + 63) // 64 * 64

        class Region:
            def __init__(self, start):
                self.at = start

            def take(self, name, shape, dt=F32):
                t = nc.alloc_sbuf_tensor_at(name, shape, dt, offset=self.at)
                self.at += (4 * int(np.prod(shape[1:])) + 31) // 32 * 32
                return t

        whole = Region(base)
        ident = whole.take("ident", [P, P])
        cos_t = whole.take("cos_t", [P, SEQ])
        sin_t = whole.take("sin_t", [P, SEQ])
        mask = whole.take("mask", [P, SEQ])
        y = whole.take("y", [P, TILES, HID])
        modT = whole.take("modT", [P, 2, CH, BATCH])
        stage = [whole.take(f"stage{i}", [P, HID]) for i in range(2)]
        hi_start = whole.at
        lo_start = hi_start + 4 * BATCH * CH * SEQ
        hT = [whole.take(f"hT_{p}", [P, BATCH * CH, SEQ], F32R) for p in ("hi", "lo")]
        wq = [whole.take(f"wq_{p}", [P, GROUP, CH, HD], F32R) for p in ("hi", "lo")]
        wk = [whole.take(f"wk_{p}", [P, CH, HD], F32R) for p in ("hi", "lo")]
        wv = [whole.take(f"wv_{p}", [P, CH, HD], F32R) for p in ("hi", "lo")]
        wo_at = whole.at
        wo = [whole.take(f"wo_{p}", [P, GROUP, HID], F32R) for p in ("hi", "lo")]
        shared = whole.at
        OT = [whole.take(f"OT_{p}", [P, GROUP, SEQ], F32R) for p in ("hi", "lo")]
        PT = [whole.take(f"PT_{p}", [P, CAUSAL], F32R) for p in ("hi", "lo")]
        probs_at = [whole.at + 4 * CAUSAL * i for i in range(3)]
        probs = [whole.take(f"probs{i}", [P, CAUSAL]) for i in range(2)]
        qT1_at = whole.at + 2 * 4 * SEQ
        qT = [[whole.take(f"qT_{p}{i}", [P, SEQ], F32R) for p in ("hi", "lo")] for i in range(2)]
        kT = [whole.take(f"kT_{p}", [P, SEQ], F32R) for p in ("hi", "lo")]
        v = [whole.take(f"v_{p}", [P, QT, HD], F32R) for p in ("hi", "lo")]
        kv_raw = whole.take("kv_raw", [P, SEQ])
        wait_slot = whole.take("wait_slot", [P, QT])
        kv_rot = whole.take("kv_rot", [P, SEQ])
        rot_c = whole.take("rot_c", [P, SEQ])
        rot_s = whole.take("rot_s", [P, SEQ])
        row_max, neg_max, row_sum, row_inv = (
            [whole.take(f"{n}{i}", [P, QT]) for i in range(2)] for n in ("row_max", "neg_max", "row_sum", "row_inv"))
        router_bias = whole.take("router_bias", [P, EXPERTS])
        small = [whole.take(f"small{i}", [P, 9]) for i in range(F_RING)]
        top8 = [whole.take(f"top8_{i}", [P, 8]) for i in range(F_RING)]
        bn6 = [whole.take(f"bn6_{i}", [P, 6]) for i in range(F_RING)]
        minus_half = whole.take("minus_half", [P, 1])
        assert whole.at <= nc.sbuf_usable_end

        hT_bytes = 4 * CH * SEQ
        after0 = Region(lo_start)
        experts = after0.take("experts", [EXPERTS, HID])
        router = after0.take("router", [P, CH, EXPERTS])
        logit, rest, weight = ([after0.take(f"{n}{i}", [P, EXPERTS]) for i in range(W_RING)]
                               for n in ("logit", "rest", "weight"))
        weightT = [after0.take(f"weightT{i}", [EXPERTS, P]) for i in range(W_RING)]
        assert after0.at <= lo_start + hT_bytes
        after1 = Region(lo_start + hT_bytes)
        after2 = Region(lo_start + 2 * hT_bytes)
        h2 = [(after1 if i < F_RING - 1 else after2).take(f"h2_{i}", [P, HID]) for i in range(F_RING)]
        gate1, shift2, scale2, gate2 = [], [], [], []
        for b in range(BATCH):
            under = Region(hi_start + b * hT_bytes)
            for tiles, n in ((gate1, "gate1"), (shift2, "shift2"), (scale2, "scale2"), (gate2, "gate2")):
                tiles.append(under.take(f"{n}_{b}", [P, HID]))
        x_in, h2T = stage[0], stage[1]

        under_OT = Region(shared)
        under_wo = Region(wo_at)
        wdk_in = Region(shared + 4 * CH * HID).take("wdk_in", [P, CH, HID])
        wdk = [under_OT.take(f"wdk_{p}", [P, CH, HID], F32R) for p in ("hi", "lo")]
        wup_hi = under_wo.take("wup_hi", [P, CH, 2 * KVC], F32R)
        wup_lo = [r.take(f"wup_lo{i}", [P, CH, 2 * KVC], F32R) for i, r in enumerate((under_wo, under_OT))]
        wup_in = [Region(at).take(f"wup_in{i}", [P, CH, 2 * KVC])
                  for i, at in enumerate((wo_at + 4 * CH * 2 * KVC, shared + 2 * 4 * CH * HID))]
        wc_out = [r.take(f"wc_out{i}", [P, 2 * KVC]) for i, r in enumerate((under_OT, under_OT, under_wo, under_wo))]
        assert under_OT.at <= probs_at[0] and under_wo.at <= shared
        under_probs0 = Region(probs_at[0])
        modrow = under_probs0.take("modrow", [BATCH, 2, HID])
        assert under_probs0.at <= probs_at[1]
        under_probs1 = Region(probs_at[1])
        h_raw = [under_probs1.take(f"h_raw{i}", [P, SEQ]) for i in range(2)]
        c_in = under_probs1.take("c_in", [P, CH, BATCH])
        c_exp = under_probs1.take("c_exp", [P, CH, BATCH])
        c_silu = under_probs1.take("c_silu", [P, CH, BATCH])
        stats = under_probs1.take("stats", [P, QT, 6])
        mean_var = under_probs1.take("mean_var", [P, TILES, 2])
        ve = under_probs1.take("ve", [P, TILES])
        rstd = under_probs1.take("rstd", [P, TILES])
        power = under_probs1.take("power", [P, TILES])
        assert under_probs1.at <= probs_at[2]
        under_qT1 = Region(qT1_at)
        gate_a = under_qT1.take("gate_a", [BATCH, HID])
        gate_b = under_qT1.take("gate_b", [BATCH, HID])
        wmod = []
        for j, at in enumerate((hi_start + 2 * hT_bytes, lo_start + 2 * hT_bytes,
                                hi_start + 3 * hT_bytes, lo_start + 3 * hT_bytes)):
            wmod.append(Region(at).take(f"wmod{j}", [P, CH, HID]))
        wmod += wmod[0:2]

        bank = {n: ctx.enter_context(nc.psum_tensor(f"bank_{n}", [P, 512], F32))
                for n in ("ta", "tb", "s3", "s2", "s1", "q", "pv", "x")}

        wc_d = nc.dram_tensor("wc_scratch", [KV, P, CH, KVC], F32).ap()
        mod_d = nc.dram_tensor("mod_scratch", [4, BATCH, HID], F32).ap()

        def passes(hi_lo_a, hi_lo_b):
            return [(hi_lo_a[0], hi_lo_b[1]), (hi_lo_a[1], hi_lo_b[0]), (hi_lo_a[0], hi_lo_b[0])]

        d_ident = count("d_ident")
        d_const, d_c, d_wdk = count("d_const"), count("d_c"), count("d_wdk")
        d_x = [count(f"d_x{b}") for b in range(BATCH)]
        d_wmod = [count(f"d_wmod{j}") for j in range(6)]
        d_wup = [count(f"d_wup{i}") for i in range(2)]
        d_wc = [count(f"d_wc{i}") for i in range(4)]
        d_mod = [count(f"d_mod{i}") for i in range(2)]
        pe_mod, pe_comb, pe_xt, pe_modT = count("pe_mod"), count("pe_comb"), count("pe_xt"), count("pe_modT")
        act_pro, act_comb, act_h = count("act_pro"), count("act_comb"), count("act_h")
        dve_pro, dve_mod, dve_ln, dve_xn, dve_h = (count("dve_pro"), count("dve_mod"), count("dve_ln"),
                                                   count("dve_xn"), count("dve_h"))
        pool_ln, pool_h = count("pool_ln"), count("pool_h")
        split_w, split_lo = count("split_w"), count("split_lo")

        x_tiles = A["x"].rearrange("(b j p) n -> b p j n", p=P, j=QT)
        wmod_v = A["wmod"].rearrange("(c p) (j n) -> j p c n", p=P, n=HID)

        def load_wmod(j):
            if j >= 4:
                pe_mod.wait(sp, j - 3)
            d_wmod[j].up(sp.dma_start(wmod[j][:], wmod_v[j]), 16)

        def load_wup(n):
            if n >= 2:
                pe_comb.wait(sp, CH * (n - 1))
            d_wup[n % 2].up(sp.dma_start(wup_in[n % 2][:], A["wup"][n]), 16)

        def load_x(b):
            d_x[b].up(sp.dma_start(y[:, QT * b:QT * b + QT, :], x_tiles[b]), 16)

        d_c.up(act.dma_start(c_in[:], A["c"]), 16)
        load_wmod(0)
        d_wdk.up(sp.dma_start(wdk_in[:], A["wdk"].rearrange("(c p) n -> p c n", p=P)), 16)
        d_ident.up(act.dma_start(ident[:], A["ident"]), 16)
        load_wup(0)
        load_wmod(1)
        load_x(0)
        load_wup(1)
        load_x(1)
        load_wmod(2)
        load_wmod(3)

        d_c.wait(act)
        act_pro.up(act.activation(c_exp[:], c_in[:], ACT.Exp, scale=-1.0))
        act_pro.wait(dve)
        n = dve_pro.up(dve.tensor_scalar(c_exp[:], c_exp[:], 1.0, None, ALU.add))
        dve_pro.wait(dve, n)
        n = dve_pro.up(dve.reciprocal(c_exp[:], c_exp[:]))
        dve_pro.wait(dve, n)
        silu_ready = dve_pro.up(dve.tensor_tensor(c_silu[:], c_in[:], c_exp[:], ALU.mult))
        dve_pro.up(dve.memset(power[:], -0.5))
        power_ready = dve_pro.value

        def modulation(j):
            ps = bank["ta" if j % 2 == 0 else "tb"]
            dve_pro.wait(pe, silu_ready)
            d_wmod[j].wait(pe, 16)
            if j >= 2:
                dve_mod.wait(pe, mod_read[j - 2])
            for c in range(CH):
                mm = pe.matmul(ps[0:BATCH, :], c_silu[:, c, :], wmod[j][:, c, :], start=(c == 0), stop=(c == CH - 1))
            pe_mod.up(mm)

        def keep_modulation(j):
            ps = bank["ta" if j % 2 == 0 else "tb"]
            pe_mod.wait(dve, j + 1)
            where = modrow[:, j % 2, :]
            if j in (2, 3):
                pe_modT.wait(dve, 1)
            if j >= 4:
                dve.wait_ge(d_mod[j % 2].sem, 16)
            if j in (0, 3):
                mod_read.append(dve_mod.up(dve.tensor_copy(where, ps[0:BATCH, :])))
            elif j in (1, 4):
                mod_read.append(dve_mod.up(dve.tensor_scalar(where, ps[0:BATCH, :], 1.0, None, ALU.add)))
            else:
                if j == 5:
                    dve_mod.wait(dve, gate_read[0])
                dve_mod.up(dve.tensor_scalar(gate_a[:], ps[0:BATCH, :], 0.0, 2.0, ALU.is_ge, ALU.mult))
                dve_mod.wait(dve)
                mod_read.append(dve_mod.up(dve.scalar_tensor_tensor(
                    out=gate_b[:], in0=gate_a[:], scalar=-1.0, in1=ps[0:BATCH, :], op0=ALU.add, op1=ALU.mult)))
                dve_mod.wait(dve)
                dve_mod.up(dve.tensor_scalar(gate_b[:], gate_b[:], 0.25, None, ALU.max))
                dve_mod.wait(dve)
                gate_read.append(dve_mod.up(dve.scalar_tensor_tensor(
                    out=where, in0=gate_a[:], scalar=-1.0, in1=gate_b[:], op0=ALU.add, op1=ALU.mult)))
            mod_done.append(dve_mod.value)

        def store_modulation(j):
            act.wait_ge(dve_mod.sem, mod_done[j])
            d_mod[j % 2].up(act.dma_start(mod_d[j - 2], modrow[:, j % 2, :]), 16)

        mod_read, mod_done, gate_read = [], [], []

        def transpose_modulation():
            dve_mod.wait(pe)
            d_ident.wait(pe)
            for j in range(2):
                for c in range(CH):
                    o = (j * CH + c) * BATCH
                    mm = pe.transpose(bank["q"][:, o:o + BATCH], modrow[:, j, c * P:(c + 1) * P],
                                      ident[0:BATCH, 0:BATCH])
            pe_modT.up(mm)
            pe_modT.wait(dve)
            modT_ready.append(dve_pro.up(dve.tensor_copy(modT[:].rearrange("p j c b -> p (j c b)"),
                                                         bank["q"][:, 0:2 * CH * BATCH])))

        modT_ready = []

        def statistics(b):
            d_x[b].wait(dve, 16)
            for j in range(QT):
                m = dve.bn_stats(stats[:, j, :], y[:, QT * b + j, :])
            dve_ln.up(m)
            dve_ln.wait(dve)
            for j in range(QT):
                m = dve.bn_aggr(mean_var[:, QT * b + j, :], stats[:, j, :])
            dve_ln.up(m)
            dve_ln.wait(pool)
            dve_pro.wait(pool, power_ready)
            s = slice(QT * b, QT * b + QT)
            n = pool_ln.up(pool.tensor_scalar(ve[:, s], mean_var[:, s, 1], EPS, None, ALU.add))
            pool_ln.wait(pool, n)
            pool_ln.up(pool.tensor_tensor(rstd[:, s], ve[:, s], power[:, s], ALU.pow))

        def normalise_x(b):
            pool_ln.wait(dve, 2 * (b + 1))
            for j in range(QT):
                i = QT * b + j
                m = dve.tensor_scalar(y[:, i, :], y[:, i, :], mean_var[:, i, 0:1], rstd[:, i:i + 1],
                                      ALU.subtract, ALU.mult)
            dve_xn.up(m)

        def transpose_h(n):
            b, c = n // CH, n % CH
            ps = bank["s1" if n % 2 == 0 else "pv"]
            dve_xn.wait(pe, b + 1)
            if n >= 2:
                dve_h.wait(pe, n - 1)
            for j in range(QT):
                mm = pe.transpose(ps[:, j * P:(j + 1) * P], y[:, QT * b + j, c * P:(c + 1) * P], ident[:])
            pe_xt.up(mm)
            pe_xt.wait(dve, n + 1)
            if n == 0:
                dve_pro.wait(dve, modT_ready[0])
            if n >= 2:
                pool_h.wait(dve, n - 1)
            dve_h.up(dve.tensor_scalar(h_raw[n % 2][:], ps[:], modT[:, 1, c, b:b + 1], modT[:, 0, c, b:b + 1],
                                       ALU.mult, ALU.add))
            dve_h.wait(act, n + 1)
            if c == 0 and b >= 2:
                pe_mod.wait(act, 6 if b == 2 else 4)
            act_h.up(act.activation(hT[0][:, n, :], h_raw[n % 2][:], ACT.Copy))
            act_h.wait(pool, n + 1)
            pool_h.up(pool.tensor_tensor(hT[1][:, n, :], h_raw[n % 2][:], hT[0][:, n, :].bitcast(F32),
                                         ALU.subtract))

        def split_down():
            d_wdk.wait(act, 16)
            for m in range(CH):
                split_w.up(act.activation(wdk[0][:, m, :], wdk_in[:, m, :], ACT.Copy))
                split_w.wait(dve)
                w = dve.tensor_tensor(wdk[1][:, m, :], wdk_in[:, m, :], wdk[0][:, m, :].bitcast(F32),
                                      ALU.subtract)
            split_lo.up(w)

        def split_up(n):
            lo = wup_lo[n % 2]
            act.wait_ge(d_wup[n % 2].sem, 16 * (n // 2 + 1))
            pe_comb.wait(act, CH * n)
            split_w.up(act.activation(wup_hi[:], wup_in[n % 2][:], ACT.Copy))
            split_w.wait(dve)
            split_lo.up(dve.tensor_tensor(lo[:], wup_in[n % 2][:], wup_hi[:].bitcast(F32), ALU.subtract))

        def combine(i):
            n, c = i // CH, i % CH
            ps = bank[COMBINE_BANKS[i]]
            if c == 0:
                split_lo.wait(pe, n + 2)
            if i >= 2:
                act_comb.wait(pe, i - 1)
            for m in range(CH):
                for k, (down, up) in enumerate(passes(wdk, (wup_hi, wup_lo[n % 2]))):
                    mm = pe.matmul(ps[:, 0:2 * KVC], down[:, m, c * P:(c + 1) * P], up[:, m, :],
                                   start=(m == 0 and k == 0), stop=(m == CH - 1 and k == 2))
            pe_comb.up(mm)
            pe_comb.wait(act, i + 1)
            if i >= 4:
                act.wait_ge(d_wc[i % 4].sem, 16 * (i // 4))
            act_comb.up(act.activation(wc_out[i % 4][:], ps[:, 0:2 * KVC], ACT.Copy))
            act_comb.wait(sp, i + 1)
            d_wc[i % 4].up(sp.dma_start(wc_d[2 * n:2 * n + 2, :, c, :].rearrange("g p k -> p g k"),
                                        wc_out[i % 4][:].rearrange("p (g k) -> p g k", g=2)), 16)

        COMBINED = KV // 2 * CH
        COMBINE_BANKS = ["s3", "s2"] * (COMBINED // 2 - 1) + ["s3", "tb"]

        act_w = mark("act_w", 1, len(CHUNKS))
        pool_w = mark("pool_w", 1, len(CHUNKS))
        d_w = [ctx.enter_context(nc.semaphore(f"d_w{i}")) for i in range(2)]
        parts = [2 if c == "wk" else 1 for c in CHUNKS]
        FIRST = len(FIRST_CHUNKS)

        def chunk_event(i):
            return FIRST + i

        def dma_value(g, i):
            per = sum(parts[j] for j in range(i % 2, len(CHUNKS), 2))
            before = sum(parts[4 + j] for j in range(i % 2, FIRST, 2))
            local = sum(parts[j] for j in range(i % 2, i + 1, 2))
            return g * (16 * per) + 16 * (before + local)

        def first_dma_value(i):
            return 16 * sum(parts[4 + j] for j in range(i % 2, i + 1, 2))

        def chunk_load(g, name, slot, free):
            free()
            to = stage[slot]
            if name.startswith("wo"):
                src = A["wo"][bass.ts(g * GROUP + int(name[2]), P), :]
                sp.dma_start(to[:], src).then_inc(d_w[slot], 16)
            elif name.startswith("wq"):
                src = A["wq"][bass.ts(g * GROUP + int(name[2]), P), :]
                sp.dma_start(to[:], src).then_inc(d_w[slot], 16)
            elif name == "wv":
                src = wc_rows[bass.ts(g, P), :].rearrange("p (c k) -> p c k", c=CH)[:, :, NOPE:KVC]
                sp.dma_start(to[:].rearrange("p (c k) -> p c k", c=CH), src).then_inc(d_w[slot], 16)
            else:
                cols = to[:].rearrange("p (a k) -> p a k", k=2 * ROPE_HALF)
                rope = A["wkr"][bass.ts(g, P), :].rearrange("p (a k) -> p a k", k=ROPE_HALF)
                sp.dma_start(cols[:, :, 0:ROPE_HALF], rope).then_inc(d_w[slot], 16)
                nope = wc_rows[bass.ts(g, P), :].rearrange("p (c k) -> p c k", c=CH)[:, :, 0:NOPE]
                for_c = to[:].rearrange("p (c a k) -> p c a k", c=CH, a=2)[:, :, :, ROPE_HALF:2 * ROPE_HALF]
                sp.dma_start(for_c, nope.rearrange("p c (a k) -> p c a k", a=2)).then_inc(d_w[slot], 16)

        wc_rows = wc_d.rearrange("g p c k -> (g p) (c k)")

        def chunk_target(name):
            n = int(name[2]) if name[-1].isdigit() else 0
            flat = {"wo": lambda w: wo[w][:, n, :],
                    "wq": lambda w: wq[w][:, n].rearrange("p c d -> p (c d)"),
                    "wk": lambda w: wk[w][:].rearrange("p c d -> p (c d)"),
                    "wv": lambda w: wv[w][:].rearrange("p c d -> p (c d)")}[name[:2]]
            return flat(0), flat(1)

        def chunk_split(name, slot, landed, event, free):
            hi, lo = chunk_target(name)
            act.wait_ge(d_w[slot], landed)
            free()
            act_w.up(act.activation(hi, stage[slot][:], ACT.Copy))
            act_w.wait(pool, event)
            pool_w.up(pool.tensor_tensor(lo, stage[slot][:], hi.bitcast(F32), ALU.subtract))

        pe_t = mark("pe_t", 3)
        pe_s = mark("pe_s", 4)
        pe_qp = mark("pe_qp")
        pe_pv = mark("pe_pv")
        pe_v = mark("pe_v", 1, BATCH)
        pe_k = mark("pe_k", 1, BATCH)
        pe_vt = mark("pe_vt", 1, BATCH)
        pe_op = mark("pe_op", QT, BATCH)
        act_t = mark("act_t", 3)
        act_exp = mark("act_exp", 2)
        act_norm = mark("act_norm", 2)
        act_q = mark("act_q")
        act_o = mark("act_o")
        act_vraw = mark("act_vraw", 1, BATCH)
        act_v = mark("act_v", 1, BATCH)
        act_kn = mark("act_kn", 1, BATCH)
        act_k = mark("act_k", 1, BATCH)
        dve_t = mark("dve_t", 3)
        dve_s = mark("dve_s", 2)
        dve_nm = mark("dve_nm", 2)
        dve_ri = mark("dve_ri", 2)
        dve_r = mark("dve_r")
        dve_o = mark("dve_o")
        dve_v = mark("dve_v", 1, BATCH)
        dve_kr = mark("dve_kr", 1, BATCH)
        dve_y = mark("dve_y", QT, BATCH, start=1)
        pool_a = mark("pool_a")
        pool_q = mark("pool_q")
        pool_ka = mark("pool_ka", 1, BATCH)
        pool_k = mark("pool_k", 1, BATCH)

        def unit_of(t):
            return t[0], t[1] // GROUP

        def before(t, n=1):
            return t[0], t[1] - n

        def q_proj(t):
            g, k = t
            b, h = (k // GROUP) % BATCH, k % GROUP
            dve_r.wait(pe, before(t))
            if b == 0:
                i = CHUNKS.index(f"wq{h}")
                shift = 0 if k < STEPS else 1
                pool_w.wait(pe, (g, len(CHUNKS) * (shift - 1) + chunk_event(i)), 1)
            for c in range(CH):
                for n, (w, x) in enumerate(passes(wq, hT)):
                    mm = pe.matmul(bank["q"][:], w[:, h, c, :], x[:, b * CH + c, :],
                                   start=(c == 0 and n == 0), stop=(c == CH - 1 and n == 2))
            pe_qp.up(mm)

        def q_rope(t):
            pe_qp.wait(dve, t)
            pool_q.wait(dve, before(t))
            dve.tensor_tensor(rot_c[:], bank["q"][:], cos_t[:], ALU.mult)
            dve.tensor_tensor(rot_s[0:64, :], bank["q"][64:128, :], sin_t[64:128, :], ALU.mult)
            dve_r.up(dve.tensor_tensor(rot_s[64:128, :], bank["q"][0:64, :], sin_t[0:64, :], ALU.mult))
            dve_r.wait(pool, t)
            pool_a.up(pool.tensor_tensor(rot_c[:], rot_c[:], rot_s[:], ALU.add))

        def q_split(t):
            hi, lo = qT[t[1] % 2]
            pool_a.wait(act, t)
            pe_s.wait(act, before(t, 2))
            act_q.up(act.activation(hi[:], rot_c[:], ACT.Copy))
            act_q.wait(pool, t)
            pool_q.up(pool.tensor_tensor(lo[:], rot_c[:], hi[:].bitcast(F32), ALU.subtract))

        def project(u, weights, chunk):
            g, b = u
            if b % BATCH == 0:
                shift = 0 if b < BATCH else 1
                pool_w.wait(pe, (g, len(CHUNKS) * (shift - 1) + chunk_event(CHUNKS.index(chunk))), 1)
            for c in range(CH):
                for n, (w, x) in enumerate(passes(weights, hT)):
                    mm = pe.matmul(bank["x"][:], w[:, c, :], x[:, (b % BATCH) * CH + c, :],
                                   start=(c == 0 and n == 0), stop=(c == CH - 1 and n == 2))
            return mm

        def k_proj(u):
            dve_y.wait(pe, before(u, 2))
            pe_k.up(project(u, wk, "wk"))

        def v_proj(u):
            act_kn.wait(pe, u)
            pe_v.up(project(u, wv, "wv"))

        def v_raw(u):
            pe_v.wait(act, u)
            act_k.wait(act, u)
            pool_k.wait(act, u)
            act_vraw.up(act.activation(kv_raw[:], bank["x"][:], ACT.Copy))

        def k_rope(u):
            ps = bank["x"]
            pe_k.wait(dve, u)
            dve.tensor_tensor(kv_raw[:], ps[:], cos_t[:], ALU.mult)
            dve.tensor_tensor(kv_rot[0:32, :], ps[64:96, :], sin_t[64:96, :], ALU.mult)
            dve_kr.up(dve.tensor_tensor(kv_rot[64:96, :], ps[0:32, :], sin_t[0:32, :], ALU.mult))
            dve_kr.wait(pool, u)
            pool_ka.up(pool.tensor_tensor(kv_raw[:], kv_raw[:], kv_rot[:], ALU.add))

        def k_nope(u):
            pool_ka.wait(act, u)
            act.activation(kv_raw[32:64, :], bank["x"][32:64, :], ACT.Copy)
            act_kn.up(act.activation(kv_raw[96:128, :], bank["x"][96:128, :], ACT.Copy))

        def k_split(u):
            act_kn.wait(act, u)
            pe_s.wait(act, (u[0], GROUP * u[1] - 1))
            act_k.up(act.activation(kT[0][:], kv_raw[:], ACT.Copy))
            act_k.wait(pool, u)
            pool_k.up(pool.tensor_tensor(kT[1][:], kv_raw[:], kT[0][:].bitcast(F32), ALU.subtract))

        def v_transpose(u):
            act_vraw.wait(pe, u)
            for j in range(QT):
                mm = pe.transpose(bank["x"][:, j * P:(j + 1) * P], kv_raw[:, j * P:(j + 1) * P], ident[:])
            pe_vt.up(mm)

        v_flat = [w[:].rearrange("p j d -> p (j d)") for w in v]

        def v_split_hi(u):
            pe_vt.wait(act, u)
            pe_pv.wait(act, (u[0], GROUP * u[1] - 1))
            act_v.up(act.activation(v_flat[0], bank["x"][:], ACT.Copy))

        def v_split_lo(u):
            act_v.wait(dve, u)
            dve_v.up(dve.tensor_tensor(v_flat[1], bank["x"][:], v_flat[0].bitcast(F32), ALU.subtract))

        score_bank = {3: bank["s3"][:, 0:512], 2: bank["s2"][:, 0:384], 1: bank["s1"][:, 0:256],
                      0: bank["s1"][:, 256:384]}
        QUERY_ORDER = [3, 2, 1, 0]

        def scores(t, middle=lambda: None):
            pool_q.wait(pe, t)
            if t[1] % GROUP == 0:
                pool_k.wait(pe, unit_of(t))
            dve_s.wait(pe, before(t))
            for qt in QUERY_ORDER:
                for n, (q, k) in enumerate(passes(qT[t[1] % 2], kT)):
                    mm = pe.matmul(score_bank[qt], q[:, qt * P:(qt + 1) * P], k[:, 0:(qt + 1) * P],
                                   start=(n == 0), stop=(n == 2))
                pe_s.up(mm)
                if qt == 2:
                    middle()

        def row(t, qt):
            return probs[t[1] % 2][:, q_offset(qt):q_offset(qt + 1)]

        def mask_and_max(t, half):
            m = t[1] % 2
            for qt in HALVES[half]:
                if qt:
                    pe_s.wait(dve, t, 4 if qt == 1 else 4 - qt)
                    dve.memset(wait_slot[:, qt:qt + 1], 0.0)
                ins = dve.tensor_tensor_reduce(row(t, qt), score_bank[qt], mask[:, SEQ - (qt + 1) * P:], 1.0, LOWEST,
                                               ALU.add, ALU.max, row_max[m][:, qt:qt + 1])
            dve_s.up(ins)
            dve_s.wait(dve, t, half + 1)
            cols = slice(HALVES[half][1], HALVES[half][0] + 1)
            dve_nm.up(dve.tensor_scalar(neg_max[m][:, cols], row_max[m][:, cols], -SCALE, None, ALU.mult))

        def exponentials(t, half):
            m = t[1] % 2
            dve_nm.wait(act, t, half + 1)
            for qt in HALVES[half]:
                ins = act.activation(row(t, qt), row(t, qt), ACT.Exp, bias=neg_max[m][:, qt:qt + 1], scale=SCALE,
                                     accum_out=row_sum[m][:, qt:qt + 1])
            act_exp.up(ins)

        def invert_sums(t, half):
            m = t[1] % 2
            cols = slice(HALVES[half][1], HALVES[half][0] + 1)
            act_exp.wait(dve, t, half + 1)
            dve_ri.up(dve.reciprocal(row_inv[m][:, cols], row_sum[m][:, cols]))

        def normalise(t, half):
            dve_ri.wait(act, t, half + 1)
            for qt in HALVES[half]:
                ins = act.activation(row(t, qt), row(t, qt), ACT.Copy, scale=row_inv[t[1] % 2][:, qt:qt + 1])
            act_norm.up(ins)

        T_PARTS = [("ta", [0]), ("tb", [1, 3]), ("ta", [2])]

        def transpose_part(t, n):
            name, keys = T_PARTS[n]
            start = KEY_OFFSET[keys[0]]
            if n == 0:
                act_norm.wait(pe, t, 1)
                dve_t.wait(pe, before(t))
            if n == 2:
                dve_t.wait(pe, t, 1)
            for kb in keys:
                for qt in reversed(range(kb, QT)):
                    if n == 0 and qt == 1:
                        act_norm.wait(pe, t, 2)
                    o = KEY_OFFSET[kb] - start + (qt - kb) * P
                    mm = pe.transpose(bank[name][:, o:o + P], row(t, qt)[:, kb * P:(kb + 1) * P], ident[:])
            pe_t.up(mm)

        def part_range(n):
            keys = T_PARTS[n][1]
            start = KEY_OFFSET[keys[0]]
            return start, sum((QT - kb) * P for kb in keys)

        def split_part_hi(t, n):
            at, size = part_range(n)
            pe_t.wait(act, t, n + 1)
            act_t.up(act.activation(PT[0][:, at:at + size], bank[T_PARTS[n][0]][:, 0:size], ACT.Copy))

        def split_part_lo(t, n):
            at, size = part_range(n)
            act_t.wait(dve, t, n + 1)
            dve_t.up(dve.tensor_tensor(PT[1][:, at:at + size], bank[T_PARTS[n][0]][:, 0:size],
                                       PT[0][:, at:at + size].bitcast(F32), ALU.subtract))

        def split_part(t, n):
            split_part_hi(t, n)
            split_part_lo(t, n)

        def values(t):
            h = t[1] % GROUP
            dve_t.wait(pe, t)
            if h == 0:
                dve_v.wait(pe, unit_of(t))
                dve_y.wait(pe, before(unit_of(t)), 3)
            else:
                dve_o.wait(pe, before(t))
            for kb in KEY_ORDER:
                for n, (a, p) in enumerate(passes(v, PT)):
                    mm = pe.matmul(bank["pv"][:, kb * P:SEQ], a[:, kb, :],
                                   p[:, KEY_OFFSET[kb]:KEY_OFFSET[kb] + (QT - kb) * P],
                                   start=(kb == 0 and n == 0), stop=(kb == KEY_ORDER[-1] and n == 2))
            pe_pv.up(mm)

        def o_split_hi(t):
            pe_pv.wait(act, t)
            act_o.up(act.activation(OT[0][:, t[1] % GROUP, :], bank["pv"][:], ACT.Copy))

        def o_split_lo(t):
            h = t[1] % GROUP
            act_o.wait(dve, t)
            dve_o.up(dve.tensor_tensor(OT[1][:, h, :], bank["pv"][:], OT[0][:, h, :].bitcast(F32), ALU.subtract))

        def out_proj(u, last=False, tiles=range(QT)):
            dve_o.wait(pe, (u[0], GROUP * u[1] + GROUP - 1))
            if u[1] == 0:
                pool_w.wait(pe, (u[0], chunk_event(3)), 1)
            for j in tiles:
                ps = bank["pv" if j % 2 == 0 else "x"]
                if j == 1 and not last:
                    dve_v.wait(pe, (u[0], u[1] + 1))
                if j >= 2:
                    dve_y.wait(pe, u, j - 1)
                if last:
                    pe.matmul(ps[:], ident[:], y[:, TILES - QT + j, :], start=True, stop=False)
                for h in range(GROUP):
                    for n, (o, w) in enumerate(passes(OT, wo)):
                        mm = pe.matmul(ps[:], o[:, h, j * P:(j + 1) * P], w[:, h, :],
                                       start=(h == 0 and n == 0 and not last), stop=(h == GROUP - 1 and n == 2))
                pe_op.up(mm)

        def add_out(u, tiles=range(QT)):
            for j in tiles:
                ps = bank["pv" if j % 2 == 0 else "x"]
                i = (u[1] % BATCH) * QT + j
                pe_op.wait(dve, u, j + 1)
                dve_y.up(dve.tensor_tensor(y[:, i, :], ps[:], y[:, i, :], ALU.add))

        def gate_out(j):
            ps = bank["pv" if j % 2 == 0 else "x"]
            pe_op.wait(dve, last_unit, j + 1)
            if j == 0:
                d_rows[BATCH - 1].wait(dve, 64)
            dve_y.up(dve.tensor_tensor(y[:, TILES - QT + j, :], ps[:], gate1[BATCH - 1][:], ALU.mult))

        final, last_unit = (KV - 1, STEPS - 1), (KV - 1, BATCH - 1)

        class Tiles:

            def __init__(self, name):
                self.sem = ctx.enter_context(nc.semaphore(name))

            def up(self, instruction):
                instruction.then_inc(self.sem, 1)

            def wait(self, engine, i):
                if i >= 0:
                    engine.wait_ge(self.sem, min(i, TILES - 1) + 1)

        (gated, x1, stat, aggregated, with_eps, root, normed, scaled, shifted, transposed, h2T_copy, logits_done,
         bias, minus_max, exp_done, top_done, replaced, chosen, weighed, wT, wT_copy, mix_done, mixed, gated2,
         out_done) = (Tiles(f"f_{n}") for n in (
             "gated", "x1", "stat", "aggregated", "with_eps", "root", "normed", "scaled", "shifted", "transposed",
             "h2T", "logits", "bias", "minus_max", "exp", "top", "replaced", "chosen", "weighed", "wT", "wT_copy",
             "mix", "mixed", "gated2", "out"))
        dve_end = count("dve_end")
        d_xin, d_router = count("d_xin"), count("d_router")
        d_rows = [count(f"d_rows{b}") for b in range(BATCH)]
        d_out = [count(f"d_out{i}") for i in range(F_RING)]
        x_rows = A["x"].rearrange("(i p) n -> i p n", p=P)
        out_rows = out.rearrange("(i p) n -> i p n", p=P)

        def real(stage):
            def run(i, *args):
                if 0 <= i < TILES:
                    stage(i, *args)
            return run

        @real
        def ffn_load(i):
            b = i // QT
            if i == 0:
                pool_w.wait(sp, (KV - 1, chunk_event(3)), 1)
                pe_qp.wait(sp, (KV - 1, GROUP - 1))
                d_router.up(sp.dma_start(experts[:], A["eb"]), 16)
                d_router.up(sp.dma_start(router[:], A["rw"]), 16)
                d_router.up(sp.dma_start(router_bias[:], A["rb"].broadcast_to([P, EXPERTS])), 16)
            x1.wait(sp, i - 1)
            d_xin.up(sp.dma_start(x_in[:], x_rows[i]), 16)
            if i % QT == 0:
                load_rows(b + 1)

        def load_rows(b):
            if b < BATCH:
                pe_qp.wait(sp, (KV - 1, GROUP * b + GROUP - 1))
                for n, tiles in enumerate((gate1, shift2, scale2, gate2)):
                    d_rows[b].up(sp.dma_start(tiles[b][:], mod_d[n, b:b + 1, :].broadcast_to([P, HID])), 16)

        @real
        def ffn_gate(i):
            b, j = i // QT, i % QT
            if b == BATCH - 1:
                return
            d_rows[b].wait(pool, 64)
            dve_y.wait(pool, (KV - 1, b), j + 1)
            gated.up(pool.tensor_tensor(y[:, i, :], y[:, i, :], gate1[b][:], ALU.mult))

        @real
        def ffn_x1(i):
            if i < TILES - QT:
                gated.wait(dve, i)
            else:
                dve_y.wait(dve, last_unit, i - (TILES - QT) + 1)
            d_xin.wait(dve, 16 * (i + 1))
            x1.up(dve.tensor_tensor(y[:, i, :], y[:, i, :], x_in[:], ALU.add))

        @real
        def ffn_stats(i):
            m = i % F_RING
            x1.wait(dve, i)
            mixed.wait(dve, i - F_RING)
            stat.up(dve.bn_stats(bn6[m][:], y[:, i, :]))
            stat.wait(dve, i)
            aggregated.up(dve.bn_aggr(small[m][:, 0:2], bn6[m][:]))
            aggregated.wait(pool, i)
            with_eps.up(pool.tensor_scalar(small[m][:, 2:3], small[m][:, 1:2], EPS, None, ALU.add))
            with_eps.wait(pool, i)
            root.up(pool.tensor_tensor(small[m][:, 3:4], small[m][:, 2:3], minus_half[:], ALU.pow))

        def norm_ready(i):
            b, m = i // QT, i % F_RING
            if i in (0, F_RING - 1):
                pe_qp.wait(dve, (KV - 1, (2 if i == 0 else 3) * GROUP - 1))
            if i >= F_RING:
                d_out[m].wait(dve, 16 * (i // F_RING))

        @real
        def ffn_norm(i):
            b, m = i // QT, i % F_RING
            norm_ready(i)
            root.wait(dve, i)
            normed.up(dve.tensor_scalar(h2[m][:], y[:, i, :], small[m][:, 0:1], small[m][:, 3:4],
                                        ALU.subtract, ALU.mult))
            normed.wait(pool, i)
            scaled.up(pool.tensor_tensor(h2[m][:], h2[m][:], scale2[b][:], ALU.mult))
            scaled.wait(pool, i)
            shifted.up(pool.tensor_tensor(h2[m][:], h2[m][:], shift2[b][:], ALU.add))

        @real
        def ffn_center(i):
            b, m = i // QT, i % F_RING
            norm_ready(i)
            if i % QT == 0:
                d_rows[b].wait(dve, 64)
            aggregated.wait(dve, i)
            shifted.wait(dve, i - 1)
            scaled.up(dve.scalar_tensor_tensor(out=h2[m][:], in0=y[:, i, :], scalar=small[m][:, 0:1],
                                               in1=scale2[b][:], op0=ALU.subtract, op1=ALU.mult))

        @real
        def ffn_shift(i):
            b, m = i // QT, i % F_RING
            root.wait(dve, i)
            scaled.wait(dve, i)
            shifted.up(dve.scalar_tensor_tensor(out=h2[m][:], in0=h2[m][:], scalar=small[m][:, 3:4],
                                                in1=shift2[b][:], op0=ALU.mult, op1=ALU.add))

        @real
        def ffn_transpose(i, ps):
            shifted.wait(pe, i)
            for c in range(CH):
                mm = pe.transpose(bank[ps][:, c * P:(c + 1) * P], h2[i % F_RING][:, c * P:(c + 1) * P], ident[:])
            transposed.up(mm)

        @real
        def ffn_h2T(i, ps):
            transposed.wait(act, i)
            logits_done.wait(act, i - 1)
            h2T_copy.up(act.activation(h2T[:], bank[ps][:], ACT.Copy))

        @real
        def ffn_logits(i, ps):
            h2T_copy.wait(pe, i)
            d_router.wait(pe, 48)
            for c in range(CH):
                mm = pe.matmul(bank[ps][:, 0:EXPERTS], h2T[:, c * P:(c + 1) * P], router[:, c, :],
                               start=(c == 0), stop=(c == CH - 1))
            logits_done.up(mm)

        @real
        def ffn_bias(i, ps):
            s, w = small[i % F_RING], i % W_RING
            logits_done.wait(dve, i)
            chosen.wait(dve, i - W_RING)
            d_router.wait(dve, 48)
            bias.up(dve.tensor_tensor_reduce(logit[w][:], bank[ps][:, 0:EXPERTS], router_bias[:], 1.0, LOWEST,
                                             ALU.add, ALU.max, s[:, 4:5]))

        @real
        def ffn_minus_max(i):
            s = small[i % F_RING]
            bias.wait(dve, i)
            minus_max.up(dve.tensor_scalar(s[:, 5:6], s[:, 4:5], -1.0, None, ALU.mult))

        @real
        def ffn_exp(i):
            s, w = small[i % F_RING], i % W_RING
            minus_max.wait(act, i)
            exp_done.up(act.activation(logit[w][:], logit[w][:], ACT.Exp, bias=s[:, 5:6], accum_out=s[:, 6:7]))

        @real
        def ffn_largest(i):
            s, w = small[i % F_RING], i % W_RING
            exp_done.wait(dve, i)
            dve.reciprocal(s[:, 7:8], s[:, 6:7])
            top_done.up(dve.max(top8[i % F_RING][:], logit[w][:]))

        @real
        def ffn_replace(i):
            w = i % W_RING
            top_done.wait(dve, i)
            weighed.wait(dve, i - W_RING)
            replaced.up(dve.match_replace(rest[w][:], top8[i % F_RING][:], logit[w][:], 0.0))

        @real
        def ffn_choose(i):
            w = i % W_RING
            replaced.wait(dve, i)
            chosen.up(dve.tensor_tensor(rest[w][:], logit[w][:], rest[w][:], ALU.subtract))

        @real
        def ffn_weigh(i):
            s, w = small[i % F_RING], i % W_RING
            chosen.wait(dve, i)
            wT.wait(dve, i - W_RING)
            weighed.up(dve.tensor_scalar(weight[w][:], rest[w][:], s[:, 7:8], 0.0, ALU.mult, ALU.add,
                                         accum_out=s[:, 8:9]))

        def ffn_top(i):
            for stage_ in (ffn_largest, ffn_replace, ffn_choose, ffn_weigh):
                stage_(i)

        @real
        def ffn_weights_T(i, ps):
            weighed.wait(pe, i)
            wT.up(pe.transpose(bank[ps][0:EXPERTS, 0:P], weight[i % W_RING][:], ident[:]))

        @real
        def ffn_weights_copy(i, ps):
            wT.wait(act, i)
            mix_done.wait(act, i - W_RING)
            wT_copy.up(act.activation(weightT[i % W_RING][:], bank[ps][0:EXPERTS, 0:P], ACT.Copy))

        @real
        def ffn_mix(i, ps):
            wT_copy.wait(pe, i)
            mix_done.up(pe.matmul(bank[ps][:], weightT[i % W_RING][:], experts[:], start=True, stop=True))

        @real
        def ffn_out(i, ps, by=pool):
            b, m = i // QT, i % F_RING
            mix_done.wait(dve, i)
            shifted.wait(dve, i)
            mixed.up(dve.scalar_tensor_tensor(out=h2[m][:], in0=h2[m][:], scalar=small[m][:, 8:9],
                                              in1=bank[ps][:], op0=ALU.mult, op1=ALU.add))
            if by is pool:
                mixed.wait(pool, i)
                gated2.up(pool.tensor_tensor(h2[m][:], h2[m][:], gate2[b][:], ALU.mult))
                gated2.wait(pool, i)
                out_done.up(pool.tensor_tensor(h2[m][:], h2[m][:], y[:, i, :], ALU.add))
                out_done.wait(sp, i)
            else:
                mixed.wait(dve, i)
                dve_end.up(dve.tensor_tensor(h2[m][:], h2[m][:], gate2[b][:], ALU.mult))
                dve_end.wait(dve)
                dve_end.up(dve.tensor_tensor(h2[m][:], h2[m][:], y[:, i, :], ALU.add))
                dve_end.wait(sp)
            d_out[m].up(sp.dma_start(out_rows[i], h2[m][:]), 16)

        def step(g, k, last=False, first=False):
            t, u = (g, k), (g, k // GROUP)
            h = k % GROUP
            has1, has3 = not last or k + 1 < STEPS, not last or k + 3 < STEPS
            more = not last or u[1] + 1 < BATCH
            nxt1, nxt3, prev, un = (g, k + 1), (g, k + 3), (g, k - 1), (g, u[1] + 1)
            nxt2 = (g, k + 2)
            has2 = not last or k + 2 < STEPS
            n = k - GROUP - 1 if last and k > GROUP else None

            transpose_part(t, 0)
            transpose_part(t, 1)
            if has1:
                if n is not None:
                    bias.wait(pe, n - 3)
                    wT_copy.wait(pe, n - 4)
                    mixed.wait(pe, n - 5)
                scores(nxt1, middle=lambda: transpose_part(t, 2))
            else:
                transpose_part(t, 2)
            if has3:
                if n is not None:
                    h2T_copy.wait(pe, n - 2)
                q_proj(nxt3)
            if h == 0 and not first:
                out_proj(before(u))
            if more and h == 1:
                k_proj(un)
            if more and h == 2:
                v_proj(un)
            if more and h == 3:
                v_transpose(un)
            if n is not None and has3:
                dve_s.wait(pe, nxt1)
                ffn_logits(n - 2, "s2")
                ffn_weights_T(n - 3, "s1")
                ffn_mix(n - 4, "s3")
            elif n is not None:
                if k == STEPS - 3:
                    dve_y.wait(pe, before(u))
                bias.wait(pe, n - 3)
                ffn_logits(n - 2, "x")
            if first:
                dve_h.wait(pe)
            values(t)
            if n is not None and not has3:
                dve_s.wait(pe, nxt1 if has1 else t)
                ffn_mix(n - 4, "s3")
                ffn_weights_T(n - 3, "s1")
            if n is not None:
                dve_r.wait(pe, nxt3 if has3 else final)
                h2T_copy.wait(pe, n - 2)
                ffn_transpose(n - 1, "q")

            split_part(t, 0)
            split_part_hi(t, 1)
            short = h == 3 and has3
            if not short:
                split_part_lo(t, 1)
            if n is not None:
                ffn_exp(n - 3)
                ffn_h2T(n - 2, "q")
            if not first:
                o_split_hi(prev)
            if h == 0:
                v_split_hi(u)
            if more and h == 2:
                k_nope(un)
            if more and h == 3:
                v_raw(un)
            if has2 and not first:
                q_split(nxt2)
            if has1:
                mask_and_max(nxt1, 0)
            if short:
                split_part_lo(t, 1)
            split_part(t, 2)
            if has1:
                exponentials(nxt1, 0)
            o_early = h == 0 or not has3
            if not first and o_early:
                o_split_lo(prev)
            if n is not None:
                ffn_norm(n - 1)
            if has1:
                mask_and_max(nxt1, 1)
            if not o_early:
                o_split_lo(prev)
            if h == 0:
                v_split_lo(u)
            if more and h == 2:
                k_split(un)
            if has1:
                exponentials(nxt1, 1)
                invert_sums(nxt1, 0)
                normalise(nxt1, 0)
            if n is not None:
                ffn_top(n - 3)
            if has1:
                invert_sums(nxt1, 1)
                normalise(nxt1, 1)
            split_chunks(g, k, last)
            if has3:
                q_rope(nxt3)
            if more and h == 1:
                k_rope(un)
            if h == 0 and not first:
                add_out(before(u))
            if last and k == STEPS - 1:
                o_split_hi(t)
                o_split_lo(t)
            if n is not None:
                ffn_bias(n - 2, "s2" if has3 else "x")
                ffn_minus_max(n - 2)
                ffn_weights_copy(n - 3, "s1")
                if has1:
                    ffn_out(n - 4, "s3")
                ffn_x1(n)
                ffn_stats(n)
            if last and k >= GROUP:
                ffn_gate(k - GROUP)
                ffn_load(k - GROUP)
            if not has1:
                ffn_out(n - 4, "s3")

        def split_chunks(g, k, last):
            for i in CHUNK_STEP.get(k, []):
                name = CHUNKS[i]
                if last and i >= 4:
                    continue

                def free(name=name):
                    if name[:2] == "wo":
                        pe_pv.wait(act, (g, 0))
                    elif name == "wv":
                        pe_v.wait(act, (g, BATCH - 1))
                    elif name == "wk":
                        pe_k.wait(act, (g, BATCH - 1))
                    else:
                        pe_qp.wait(act, (g, STEPS - GROUP + int(name[2])))
                chunk_split(name, i % 2, dma_value(g, i), (g, chunk_event(i)), free)

        def group_loads(g, last=False):
            for i, name in enumerate(CHUNKS):
                if last and i >= 4:
                    break

                def stage_free(i=i):
                    pool_w.wait(sp, (g, chunk_event(i) - 2), 1)
                chunk_load(g if i < 4 else g + 1, name, i % 2, stage_free)

        zero = (0, 0)
        rot_clear = dve_pro.up(dve.memset(kv_rot[:], 0.0))
        half_ready = dve_pro.up(dve.memset(minus_half[:], -0.5))

        def split_first(i):
            chunk_split(FIRST_CHUNKS[i], i % 2, first_dma_value(i), (0, i), lambda: None)

        def load_first(i):
            def stage_free():
                if i >= 2:
                    pool_w.wait(sp, (0, i - 2), 1)
                if FIRST_CHUNKS[i] in ("wk", "wv"):
                    for w in d_wc:
                        w.wait(sp, 16)
            chunk_load(0, FIRST_CHUNKS[i], i % 2, stage_free)

        def key_start():
            pool_h.wait(pe, CH)
            k_proj(zero)
            dve_pro.wait(dve, rot_clear)
            d_const.wait(dve, 48)
            k_rope(zero)

        def key_end():
            k_nope(zero)
            k_split(zero)

        def query(n):
            if n == 0:
                dve_pro.wait(pe, modT_ready[0])
            q_proj((0, n))
            q_rope((0, n))

        def query_end(n):
            if n == 1:
                dve_mod.wait(act, mod_done[5])
            q_split((0, n))

        def first_scores():
            act_comb.wait(pe, COMBINED - 1)
            scores(zero, middle=lambda: dve_h.wait(pe, BATCH * CH - 1))
            for w in d_mod:
                w.wait(dve, 32)
            for half in (0, 1):
                mask_and_max(zero, half)
                exponentials(zero, half)
            for half in (0, 1):
                invert_sums(zero, half)
                normalise(zero, half)

        def clear_y(b):
            pe_xt.wait(pool, CH * (b + 1))
            m = pool.memset(y[:, QT * b:QT * b + QT, :], 0.0)
            if b == BATCH - 1:
                dve_y.up(m)

        def combine_late(i):
            dve_mod.wait(pe, mod_read[5])
            combine(i)

        def load_constants():
            for dst, name in ((cos_t, "cos"), (sin_t, "sin"), (mask, "mask")):
                d_const.up(sp.dma_start(dst[:], A[name]), 16)

        C, M, K, H, W, Z = combine, modulation, keep_modulation, transpose_h, split_first, clear_y
        for stage_, *args in (
                (M, 0), (split_down,), (split_up, 0), (K, 0), (M, 1), (K, 1), (statistics, 0), (C, 0),
                (transpose_modulation,), (C, 1), (normalise_x, 0), (C, 2), (statistics, 1), (C, 3),
                (load_first, 0), (load_first, 1), (load_x, 2), (load_constants,), (split_up, 1),
                (M, 2), (H, 0), (H, 1), (C, 4), (normalise_x, 1), (H, 2), (C, 5), (W, 0), (H, 3), (K, 2), (C, 6),
                (W, 1), (H, 4), (load_first, 2), (C, 7), (load_wmod, 4), (load_wup, 2), (load_wmod, 5), (load_x, 3),
                (load_first, 3), (load_wup, 3), (load_first, 4), (load_first, 5), (H, 5), (store_modulation, 2),
                (key_start,), (W, 2), (M, 3), (H, 6), (key_end,), (K, 3), (statistics, 2), (H, 7), (split_up, 2),
                (M, 4), (W, 3), (normalise_x, 2), (store_modulation, 3), (v_proj, zero), (v_raw, zero), (K, 4), (Z, 0),
                (M, 5), (statistics, 3), (Z, 1), (v_transpose, zero),
                (C, 8), (H, 8), (store_modulation, 4), (query, 0), (K, 5), (C, 9), (H, 9), (W, 4),
                (query_end, 0), (C, 10), (H, 10), (normalise_x, 3), (C, 11), (split_up, 3), (H, 11),
                (store_modulation, 5), (query, 1), (H, 12), (H, 13), (W, 5), (query_end, 1), (C, 12), (C, 13),
                (H, 14), (C, 14), (first_scores,), (query, 2), (combine_late, 15), (H, 15), (query_end, 2)):
            stage_(*args)

        act_comb.wait(pe)
        act_h.wait(dve)
        pool_h.wait(dve)
        pe_comb.wait(act)
        for w in d_wc[0:2]:
            w.wait(act)
        dve_pro.wait(pool, half_ready)
        step(0, 0, first=True)
        pool_h.wait(pe)
        clear_y(2)
        clear_y(3)
        for w in d_wc:
            w.wait(act)
            w.wait(sp)

        with nc.Fori(0, KV - 1) as g:
            group_loads(g)
            for k in range(1, STEPS + 1):
                step(g, k)
        group_loads(KV - 1, last=True)
        load_rows(0)
        for k in range(1, STEPS):
            step(KV - 1, k, last=True)
        for n in range(TILES - GROUP - 1, TILES):
            j = n - (TILES - GROUP - 1)
            ffn_exp(n - 3)
            ffn_h2T(n - 2, "q")
            bias.wait(pe, n - 3)
            ffn_logits(n - 2, "s2")
            mixed.wait(pe, n - 5)
            ffn_mix(n - 4, "s3")
            ffn_largest(n - 3)
            ffn_replace(n - 3)
            ffn_center(n - 1)
            ffn_choose(n - 3)
            ffn_shift(n - 1)
            ffn_weigh(n - 3)
            if j:
                gate_out(j - 1)
            h2T_copy.wait(pe, n - 2)
            ffn_transpose(n - 1, "q")
            wT_copy.wait(pe, n - 4)
            ffn_weights_T(n - 3, "s1")
            if j < QT:
                out_proj(last_unit, tiles=[j], last=True)
            ffn_bias(n - 2, "s2")
            ffn_x1(n)
            ffn_load(n + 1)
            ffn_minus_max(n - 2)
            ffn_weights_copy(n - 3, "s1")
            ffn_stats(n)
            ffn_out(n - 4, "s3")
        a, b, c, d = range(TILES - QT, TILES)
        dve_y.wait(pe, last_unit, QT - 1)
        ffn_mix(a, "pv")
        ffn_exp(b)
        ffn_h2T(c, "q")
        bias.wait(pe, b)
        ffn_logits(c, "s2")
        ffn_center(d)
        ffn_largest(b)
        ffn_shift(d)
        ffn_transpose(d, "ta")
        ffn_replace(b)
        ffn_bias(c, "s2")
        ffn_choose(b)
        ffn_minus_max(c)
        ffn_weigh(b)
        ffn_h2T(d, "ta")
        wT_copy.wait(pe, a)
        ffn_weights_T(b, "s1")
        ffn_logits(d, "tb")
        ffn_exp(c)
        ffn_weights_copy(b, "s1")
        ffn_out(a, "pv")
        ffn_largest(c)
        ffn_bias(d, "tb")
        ffn_replace(c)
        ffn_minus_max(d)
        mixed.wait(pe, a - 1)
        ffn_mix(b, "s3")
        ffn_choose(c)
        ffn_exp(d)
        ffn_weigh(c)
        ffn_weights_T(c, "x")
        ffn_weights_copy(c, "x")
        ffn_largest(d)
        ffn_mix(c, "q")
        ffn_replace(d)
        ffn_choose(d)
        ffn_weigh(d)
        ffn_weights_T(d, "s2")
        ffn_weights_copy(d, "s2")
        ffn_out(b, "s3")
        ffn_out(c, "q", dve)
        ffn_mix(d, "ta")
        ffn_out(d, "ta", dve)
        for w in d_out:
            w.wait(sp)


def kernel(L0_attn_hidden_states, L0_attn_Wq, L0_attn_Wkr, L0_attn_Wdk, L0_attn_Wupk, L0_attn_Wupv, L0_attn_Wo,
           L0_ffn_router_weight, L0_ffn_router_bias, L0_ffn_expert_bias, L0_c, L0_wmod):
    import concourse.bacc as bacc
    from concourse.bass_utils import run_bass_kernel_spmd

    def lay(a, shape=None):
        a = np.ascontiguousarray(a)
        return a if shape is None else a.reshape(shape)

    upk = np.asarray(L0_attn_Wupk).reshape(KV, NOPE, HID)
    upv = np.asarray(L0_attn_Wupv).reshape(KV, HD, HID)
    up = np.concatenate([upk, upv], axis=1).reshape(KV // 2, 2 * KVC, CH, P).transpose(0, 3, 2, 1)
    inv_freq = 1.0 / 10000.0 ** (np.arange(0, HD, 2, dtype=np.float32) / HD)
    freqs = np.outer(np.arange(SEQ, dtype=np.float32), inv_freq)
    emb = np.concatenate([freqs, freqs], axis=-1)
    sign = np.concatenate([np.ones(HD // 2, np.float32), -np.ones(HD // 2, np.float32)])[:, None]
    causal = np.zeros((P, SEQ), np.float32)
    causal[:, SEQ - P:] = np.where(np.tril(np.ones((P, P), bool)), 0.0, MASKED)
    arrays = {
        "x": lay(L0_attn_hidden_states, (BATCH * SEQ, HID)),
        "c": lay(np.asarray(L0_c).T.reshape(CH, P, BATCH).transpose(1, 0, 2)),
        "wmod": lay(L0_wmod),
        "wq": lay(np.asarray(L0_attn_Wq).reshape(HEADS, HD, CH, P).transpose(0, 3, 2, 1), (HEADS * P, HID)),
        "wkr": lay(np.asarray(L0_attn_Wkr).reshape(KV, 2 * ROPE_HALF, CH, P).transpose(0, 3, 2, 1),
                   (KV * P, CH * 2 * ROPE_HALF)),
        "wdk": lay(L0_attn_Wdk),
        "wup": lay(up),
        "wo": lay(np.asarray(L0_attn_Wo).T),
        "rw": lay(np.asarray(L0_ffn_router_weight).T.reshape(CH, P, EXPERTS).transpose(1, 0, 2)),
        "rb": lay(L0_ffn_router_bias, (1, EXPERTS)),
        "eb": lay(L0_ffn_expert_bias),
        "cos": lay(np.cos(emb).astype(np.float32).T),
        "sin": lay(np.sin(emb).astype(np.float32).T * sign),
        "mask": causal,
        "ident": np.eye(P, dtype=np.float32),
    }
    nc = bacc.Bacc("TRN2", target_bir_lowering=False, num_devices=1)
    aps = {n: nc.dram_tensor(f"in_{n}", a.shape, F32, kind="ExternalInput").ap() for n, a in arrays.items()}
    out = nc.dram_tensor("out_y", (BATCH * SEQ, HID), F32, kind="ExternalOutput").ap()
    build(nc, aps, out)
    r = run_bass_kernel_spmd(nc, [{f"in_{n}": a for n, a in arrays.items()}], core_ids=[0])
    return r.results[0]["out_y"].reshape(BATCH, SEQ, HID)
```
